# Optimizing a Trainium2 kernel written in Bass

```python
import numpy as np
import jax
import jax.numpy as jnp

def _softmax(x, axis=-1):
    return jax.nn.softmax(x, axis=axis)

def _gelu(x):
    return jax.nn.gelu(x, approximate=True)

def _silu(x):
    return jax.nn.silu(x)

def _sigmoid(x):
    return jax.nn.sigmoid(x)

def _layernorm(x, axis=-1, eps=1e-05):
    m = jnp.mean(x, axis=axis, keepdims=True)
    v = jnp.var(x, axis=axis, keepdims=True)
    return (x - m) / jnp.sqrt(v + eps)

def _scatter_add(tgt, idx, src, axis=0):
    return tgt.at[idx].add(src)

def _segment_sum(src, seg, n):
    return jax.ops.segment_sum(src, seg, n)
kernel_name = 'mk_adj_preln_d2_adj_r2_453fcd'

def setup_inputs(seed: int=0):
    np.random.seed(seed)
    _w = jnp.asarray

    def _rec_inputs():
        import jax
        import jax.numpy as jnp
        _gk = jax.random.key(seed)
        x = -0.000929 + 1 * jax.random.normal(jax.random.fold_in(_gk, 1), (8192, 64), jnp.float32)
        _a = jax.random.bernoulli(jax.random.fold_in(_gk, 2), 0.000488281, (8192, 8192))
        _a = jnp.logical_or(_a, jnp.eye(8192, dtype=bool))
        _af = _a.astype(jnp.float32)
        _af = _af * jax.random.uniform(jax.random.fold_in(_gk, 3), (8192, 8192), jnp.float32, 0.05, 1)
        adj = _af
        return (x, adj)
    x, adj = _rec_inputs()

    def _L0_gnn_setup():
        import jax, jax.numpy as jnp
        import numpy as np
        N = 8192
        IN_C = 64
        OUT_C = 64
        key = jax.random.key(seed)
        k1, k2, k3 = jax.random.split(key, 3)
        x = jax.random.normal(k1, (N, IN_C), dtype=jnp.float32)
        adj = jax.random.uniform(k2, (N, N), dtype=jnp.float32)
        scale = jnp.sqrt(6.0 / (IN_C + OUT_C))
        weight = jax.random.uniform(k3, (IN_C, OUT_C), dtype=jnp.float32, minval=-scale, maxval=scale)
        return {'x': x, 'adj': adj, 'weight': weight}
    _L0_gnn_all = _L0_gnn_setup()
    _L0_gnn_in = {k: v for k, v in _L0_gnn_all.items() if k in ('weight',)}
    del _L0_gnn_all

    def _L1_gnn_setup():
        import jax, jax.numpy as jnp
        import numpy as np
        N, D = (6144, 64)

        def _ggc(x, adj, W, wih, whh, bih, bhh):
            m = adj @ (x @ W)
            gi = m @ wih.T + bih
            gh = x @ whh.T + bhh
            i_r, i_z, i_n = jnp.split(gi, 3, axis=-1)
            h_r, h_z, h_n = jnp.split(gh, 3, axis=-1)
            r = jax.nn.sigmoid(i_r + h_r)
            z = jax.nn.sigmoid(i_z + h_z)
            n = jnp.tanh(i_n + r * h_n)
            return (1.0 - z) * n + z * x
        key = jax.random.key(seed)
        ks = jax.random.split(key, 8)
        s = 1.0 / np.sqrt(D)
        return {'x': jax.random.normal(ks[0], (N, D), jnp.float32), 'adj': jax.random.uniform(ks[1], (N, N), jnp.float32), 'W1': jax.random.normal(ks[2], (D, D), jnp.float32) * s, 'wih1': jax.random.normal(ks[3], (3 * D, D), jnp.float32) * s, 'whh1': jax.random.normal(ks[4], (3 * D, D), jnp.float32) * s, 'bih1': jnp.zeros((3 * D,), jnp.float32), 'bhh1': jnp.zeros((3 * D,), jnp.float32), 'W2': jax.random.normal(ks[5], (D, D), jnp.float32) * s, 'wih2': jax.random.normal(ks[6], (3 * D, D), jnp.float32) * s, 'whh2': jax.random.normal(ks[7], (3 * D, D), jnp.float32) * s, 'bih2': jnp.zeros((3 * D,), jnp.float32), 'bhh2': jnp.zeros((3 * D,), jnp.float32)}
    _L1_gnn_all = _L1_gnn_setup()
    _L1_gnn_in = {k: v for k, v in _L1_gnn_all.items() if k in ('W1', 'wih1', 'whh1', 'bih1', 'bhh1', 'W2', 'wih2', 'whh2', 'bih2', 'bhh2')}
    del _L1_gnn_all
    return {'x': x, 'adj': adj, 'L0_gnn_weight': _L0_gnn_in['weight'], 'L1_gnn_W1': _L1_gnn_in['W1'], 'L1_gnn_wih1': _L1_gnn_in['wih1'], 'L1_gnn_whh1': _L1_gnn_in['whh1'], 'L1_gnn_bih1': _L1_gnn_in['bih1'], 'L1_gnn_bhh1': _L1_gnn_in['bhh1'], 'L1_gnn_W2': _L1_gnn_in['W2'], 'L1_gnn_wih2': _L1_gnn_in['wih2'], 'L1_gnn_whh2': _L1_gnn_in['whh2'], 'L1_gnn_bih2': _L1_gnn_in['bih2'], 'L1_gnn_bhh2': _L1_gnn_in['bhh2']}

def reference(x, adj, L0_gnn_weight, L1_gnn_W1, L1_gnn_wih1, L1_gnn_whh1, L1_gnn_bih1, L1_gnn_bhh1, L1_gnn_W2, L1_gnn_wih2, L1_gnn_whh2, L1_gnn_bih2, L1_gnn_bhh2):
    import jax
    import jax.numpy as jnp

    def _L0_gnn_ref(x, adj, weight):
        import jax, jax.numpy as jnp
        import numpy as np
        N = 8192
        IN_C = 64
        OUT_C = 64
        agg = adj @ x
        return agg @ weight

    def _L1_gnn_ref(x, adj, W1, wih1, whh1, bih1, bhh1, W2, wih2, whh2, bih2, bhh2):
        import jax, jax.numpy as jnp
        import numpy as np
        N, D = (6144, 64)

        def _ggc(x, adj, W, wih, whh, bih, bhh):
            m = adj @ (x @ W)
            gi = m @ wih.T + bih
            gh = x @ whh.T + bhh
            i_r, i_z, i_n = jnp.split(gi, 3, axis=-1)
            h_r, h_z, h_n = jnp.split(gh, 3, axis=-1)
            r = jax.nn.sigmoid(i_r + h_r)
            z = jax.nn.sigmoid(i_z + h_z)
            n = jnp.tanh(i_n + r * h_n)
            return (1.0 - z) * n + z * x
        h = jax.nn.relu(_ggc(x, adj, W1, wih1, whh1, bih1, bhh1))
        return jax.nn.relu(_ggc(h, adj, W2, wih2, whh2, bih2, bhh2))
    h = jnp.maximum(_layernorm(x, axis=-1), 0.0)
    x = x + _L0_gnn_ref(h, adj, L0_gnn_weight)
    h = jnp.maximum(_layernorm(x, axis=-1), 0.0)
    x = x + _L1_gnn_ref(h, adj, L1_gnn_W1, L1_gnn_wih1, L1_gnn_whh1, L1_gnn_bih1, L1_gnn_bhh1, L1_gnn_W2, L1_gnn_wih2, L1_gnn_whh2, L1_gnn_bih2, L1_gnn_bhh2)
    return x

_drawn_inputs = setup_inputs


def setup_inputs(seed=0):
    import zlib

    import numpy as np

    out = dict(_drawn_inputs(seed))
    spreads = {'L1_gnn_bih1': (0.0, 0.613),
     'L1_gnn_bhh1': (0.0, 0.8),
     'L1_gnn_bih2': (0.0, 0.509),
     'L1_gnn_bhh2': (0.0, 0.748)}
    factors = {}
    for name, (base, spread) in spreads.items():
        noise = np.random.default_rng([zlib.crc32(name.encode()), seed]).standard_normal(out[name].shape)
        drawn = base * np.exp(spread * noise) if base else spread * noise
        out[name] = jnp.asarray(drawn.astype(out[name].dtype))
    for name, factor in factors.items():
        out[name] = (out[name] * factor).astype(out[name].dtype)
    return out
```

```python
import numpy as np
import concourse.bass as bass
from concourse import mybir
from concourse.alu_op_type import AluOpType as ALU
from contextlib import ExitStack

N, C = 8192, 64
P = 128
B = 512
NB = N // B
KT = B // P
QUAD = 4
NQ = NB // QUAD
RAW = 4
SPL = 2
EPS = 1e-5
G = 4 * C


def build(nc, blocks, x, w0, w1, w2, wi1, wi2, wh1, wh2, ident_in, out):
    f32, f32r = mybir.dt.float32, mybir.dt.float32r
    ACT = mybir.ActivationFunctionType
    AX = mybir.AxisListType
    ctx = ExitStack()
    with ctx:
        def sb(name, shape, dt=f32):
            return ctx.enter_context(nc.sbuf_tensor(name, shape, dt))

        def pb(name, shape):
            return ctx.enter_context(nc.psum_tensor(name, shape, f32))

        def sem(name):
            return ctx.enter_context(nc.semaphore(name))

        ya = sb("ya", [P, NB, KT, 2 * C], f32r)
        yb = sb("yb", [P, NB, KT, 2 * C], f32r)
        part = sb("part", [P, NB, B])
        x1 = sb("x1", [P, NB, KT, C])
        hall = sb("hall", [P, NB, KT, C])
        raw = sb("raw", [P, RAW, KT * B])
        hi = sb("hi", [P, SPL, KT * B], f32r)
        lo = sb("lo", [P, SPL, KT * B], f32r)
        w0s = sb("w0s", [P, C])
        w1s = sb("w1s", [C, C])
        w2s = sb("w2s", [C, C])
        wi = [sb("wi1s", [P, 3 * C]), sb("wi2s", [P, 3 * C])]
        wh = [sb("wh1s", [C + 2, G]), sb("wh2s", [C + 2, G])]
        ident = sb("ident", [P, P])
        mt = sb("mt", [P, B])
        ht = sb("ht", [C + 2, B])
        hs = sb("hs", [P, KT, C])
        dev = sb("dev", [P, KT, C])
        sq = sb("sq", [P, KT, C])
        st = sb("st", [P, 5, KT])
        rz = sb("rz", [P, KT, 2 * C])
        acc_a = pb("acc_a", [P, 2, B])
        acc_b = pb("acc_b", [P, 2, B])
        ps_g = pb("ps_g", [P, KT, G])
        ps_t = pb("ps_t", [P, B])
        ps_y = pb("ps_y", [P, KT, P])

        loaded = [sem(f"loaded{s}") for s in range(RAW)]
        hi_ready = sem("hi_ready")
        lo_ready = sem("lo_ready")
        used = sem("used")
        consts_in = sem("consts_in")
        x_in = sem("x_in")
        zeroed = sem("zeroed")
        ones_set = sem("ones_set")
        ln_step = sem("ln_step")
        var_ready = sem("var_ready")
        std_ready = sem("std_ready")
        h_ready = sem("h_ready")
        y1_hi = sem("y1_hi")
        y1_ready = sem("y1_ready")
        e1_mt = sem("e1_mt")
        e1_part = sem("e1_part")
        e1_agg = sem("e1_agg")
        e1_x1 = sem("e1_x1")
        e1_t = sem("e1_t")
        e1_ht = sem("e1_ht")
        e1_kept = sem("e1_kept")
        e1_y = sem("e1_y")
        e1_yhi = sem("e1_yhi")
        y2_ready = sem("y2_ready")
        g_old = sem("g_old")
        g_oldt = sem("g_oldt")
        g_oldht = sem("g_oldht")
        g_mt = sem("g_mt")
        g_part = sem("g_part")
        g_gates = sem("g_gates")
        g_rz = sem("g_rz")
        g_step = sem("g_step")
        g_narg = sem("g_narg")
        g_n = sem("g_n")
        g_h = sem("g_h")
        g_t = sem("g_t")
        g_ht = sem("g_ht")
        g_kept = sem("g_kept")
        g_y = sem("g_y")
        g_yhi = sem("g_yhi")
        y3_ready = sem("y3_ready")
        stored = sem("stored")

        past_sp, past_dve, past_pool, past_pe = (sem(f"past_{e}") for e in ("sp", "dve", "pool", "pe"))

        block = ctx.enter_context(nc.Block())

        def runs(sweep):
            t0 = {1: 0, 2: NB * NB, 3: NB * NB + QUAD * QUAD * NQ * (NQ + 1) // 2}[sweep]
            found = []
            for s in (range(NQ) if sweep == 1 else range(NQ - 1, -1, -1)):
                quads = {1: list(range(NQ - 1, -1, -1)), 2: list(range(s, NQ)),
                         3: list(range(s, -1, -1))}[sweep]
                first, step = (QUAD * s, 1) if sweep == 1 else (QUAD * s + QUAD - 1, -1)
                cuts = [(first, QUAD)]
                if (sweep == 1 and s == 0) or (sweep > 1 and s == NQ - 1):
                    cuts = [(first, 1), (first + step, QUAD - 1)]
                for a, n in cuts:
                    found.append((s, a, step, n, quads, t0))
                    t0 += n * len(quads) * QUAD
            return found

        def ks(sweep, q):
            return range(QUAD * q + QUAD - 1, QUAD * q - 1, -1) if sweep != 2 else range(QUAD * q, QUAD * q + QUAD)

        T2 = NB * NB
        T3 = T2 + QUAD * QUAD * NQ * (NQ + 1) // 2
        T_END = 2 * T3 - T2

        def over_rows(eng, sweep, body):
            for s, a, step, n, quads, t0 in runs(sweep):
                o = a if sweep == 1 else NB - 1 - a
                if n == 1:
                    body(s, a, o, quads, t0, True)
                else:
                    with eng.Fori(0, n) as r:
                        body(s, a + step * r, o + r, quads, t0 + r * (QUAD * len(quads)), False)

        @block.sync
        def _(sp):
            def load(row, k, t, m):
                sp.wait_ge(lo_ready, t + m + 1)
                sp.sem_inc(past_sp, 1)
                sp.dma_start(raw[:, m % RAW, :], blocks[row, k, :, :]).then_inc(loaded[m % RAW], 16)

            for sweep in (1, 2, 3):
                def row_loads(s, row, o, quads, t, first):
                    m = 0
                    for q in quads:
                        for k in ks(sweep, q):
                            load(row, k, t, m)
                            m += 1
                over_rows(sp, sweep, row_loads)
            sp.wait_ge(stored, 16 * NB)

        @block.scalar
        def _(act):
            act.dma_start(x1[:, :, :, :], x).then_inc(x_in, 16)
            for dst, src in ((w0s[:C, :], w0), (w0s[C:, :], w0), (w1s[:, :], w1), (w2s[:, :], w2),
                             (wi[0][:C, :], wi1), (wi[0][C:, :], wi1), (wi[1][:C, :], wi2), (wi[1][C:, :], wi2),
                             (wh[0][:, :], wh1), (wh[1][:, :], wh2), (ident[:, :], ident_in)):
                act.dma_start(dst, src).then_inc(consts_in, 16)

            def split(t, m):
                act.wait_ge(loaded[m % RAW], (t + m - m % RAW) * (16 // RAW) + 16)
                act.wait_ge(used, t + m + 1)
                nc.scalar.copy(hi[:, m % SPL, :], raw[:, m % RAW, :]).then_inc(hi_ready, 1)

            def root(e):
                act.wait_ge(var_ready, e + 1)
                nc.scalar.activation(st[:, 3, :], st[:, 2, :], ACT.Sqrt).then_inc(std_ready, 1)

            def transposed(src_sem, n, dst_sem):
                act.wait_ge(src_sem, n)
                nc.scalar.copy(ht[:C, :], ps_t[:C, :]).then_inc(dst_sem, 1)

            def row1(s, row, o, quads, t, first):
                m = 0
                for q in quads:
                    for k in ks(1, q):
                        if first:
                            split(t, m)
                            root(m)
                            act.wait_ge(h_ready, m + 1)
                            nc.scalar.copy(ya[:, k, :, :C], hs[:, :, :]).then_inc(y1_hi, 1)
                        else:
                            if m == 2:
                                e1_part_save(o - 1, row - 1, t)
                            if m == 4:
                                root(NB + o - 1)
                            if m == 5:
                                transposed(e1_t, o, e1_ht)
                            if m == 6:
                                e1_y_hi(o - 1, row - 1)
                            split(t, m)
                        m += 1

            def e1_part_save(e, prev, t):
                act.wait_ge(used, t + SPL)
                nc.scalar.copy(part[:, prev, :], acc_b[:, prev % 2, :]).then_inc(e1_part, 1)

            def e1_y_hi(e, prev):
                act.wait_ge(e1_y, e + 1)
                nc.scalar.copy(yb[:, prev, :, :C], ps_y[:, :, :C]).then_inc(e1_yhi, 1)

            act.wait_ge(zeroed, 1)
            over_rows(act, 1, row1)
            e1_part_save(NB - 1, NB - 1, T2)
            root(2 * NB - 1)
            transposed(e1_t, NB, e1_ht)
            e1_y_hi(NB - 1, NB - 1)

            def g_sig(e):
                act.wait_ge(g_gates, e + 1)
                nc.scalar.activation(rz[:, :, :], ps_g[:, :, :2 * C], ACT.Sigmoid).then_inc(g_rz, 1)

            def g_tanh(e):
                act.wait_ge(g_narg, e + 1)
                nc.scalar.activation(sq[:, :, :], sq[:, :, :], ACT.Tanh).then_inc(g_n, 1)

            def g_part_save(e, prev, t):
                act.wait_ge(g_mt, e + 1)
                nc.scalar.copy(part[:, prev, :], acc_a[:, prev % 2, :]).then_inc(g_part, 1)

            def g_y_hi(e, prev):
                act.wait_ge(g_y, e + 1)
                nc.scalar.copy(ya[:, prev, :, :C], ps_y[:, :, :C]).then_inc(g_yhi, 1)

            def gru_rows(sweep):
                def row(s, row_, o, quads, t, first):
                    prev = row_ + 1
                    e = o - 1 if sweep == 2 else NB + o - 1
                    for m in range(QUAD * len(quads)):
                        if not first:
                            if m == 2:
                                transposed(g_oldt, e + 1, g_oldht)
                                if sweep == 2:
                                    g_part_save(e, prev, t)
                            if m == 3:
                                g_sig(e)
                                g_tanh(e)
                            if sweep == 2 and len(quads) > 1 and m == 5:
                                transposed(g_t, e + 1, g_ht)
                            if sweep == 2 and len(quads) > 1 and m == 6:
                                g_y_hi(e, prev)
                        split(t, m)
                    if sweep == 2 and len(quads) == 1 and not first:
                        transposed(g_t, e + 1, g_ht)
                        g_y_hi(e, prev)
                return row

            act.wait_ge(zeroed, 2)
            over_rows(act, 2, gru_rows(2))
            transposed(g_oldt, NB, g_oldht)
            g_part_save(NB - 1, 0, T3)
            g_sig(NB - 1)
            g_tanh(NB - 1)
            transposed(g_t, NB, g_ht)
            g_y_hi(NB - 1, 0)
            over_rows(act, 3, gru_rows(3))
            transposed(g_oldt, 2 * NB, g_oldht)
            g_sig(2 * NB - 1)
            g_tanh(2 * NB - 1)

        @block.vector
        def _(dve):
            dve.sem_inc(lo_ready, RAW)
            nc.vector.memset(acc_b[:, :, :], 0.0).then_inc(zeroed, 1)
            nc.vector.memset(ht[C:, :], 1.0).then_inc(ones_set, 1)

            def split(t, m):
                dve.wait_ge(hi_ready, t + m + 1)
                nc.vector.tensor_tensor(lo[:, m % SPL, :], raw[:, m % RAW, :], hi[:, m % SPL, :].bitcast(f32),
                                        ALU.subtract).then_inc(lo_ready, 1)

            LN_STEPS = 6

            def ln_first(e, row):
                def step(i, ins):
                    ins.then_inc(ln_step, 1)
                    dve.wait_ge(ln_step, e * LN_STEPS + i)
                step(1, nc.vector.tensor_reduce(st[:, 0, :], x1[:, row, :, :], AX.X, ALU.add))
                step(2, nc.vector.tensor_scalar(st[:, 1, :], st[:, 0, :], -1.0 / C, None, ALU.mult))
                step(3, nc.vector.tensor_tensor(dev[:, :, :], x1[:, row, :, :],
                                                st[:, 1, :].unsqueeze(2).to_broadcast([P, KT, C]), ALU.add))
                step(4, nc.vector.tensor_tensor(sq[:, :, :], dev[:, :, :], dev[:, :, :], ALU.mult))
                step(5, nc.vector.tensor_reduce(st[:, 0, :], sq[:, :, :], AX.X, ALU.add))
                nc.vector.tensor_scalar(st[:, 2, :], st[:, 0, :], 1.0 / C, EPS, ALU.mult, ALU.add).then_inc(var_ready, 1)

            def ln_second(e):
                dve.wait_ge(std_ready, e + 1)
                nc.vector.reciprocal(st[:, 4, :], st[:, 3, :]).then_inc(ln_step, 1)
                dve.wait_ge(ln_step, e * LN_STEPS + 6)
                nc.vector.scalar_tensor_tensor(out=hs[:, :, :], in0=dev[:, :, :], scalar=0.0,
                                               in1=st[:, 4, :].unsqueeze(2).to_broadcast([P, KT, C]),
                                               op0=ALU.max, op1=ALU.mult).then_inc(h_ready, 1)

            def e1_take(e, prev, t):
                dve.wait_ge(used, t + SPL)
                nc.vector.tensor_copy(mt[:, :], acc_a[:, prev % 2, :]).then_inc(e1_mt, 1)

            def e1_norm(e, prev):
                dve.wait_ge(e1_agg, e + 1)
                nc.vector.tensor_tensor(x1[:, prev, :, :], x1[:, prev, :, :], ps_y[:, :, :C], ALU.add)\
                    .then_inc(e1_x1, 1)
                dve.wait_ge(e1_x1, e + 1)
                dve.sem_inc(past_dve, 1)
                ln_first(NB + e, prev)

            def e1_hs_free(e):
                dve.wait_ge(e1_kept, e)
                dve.wait_ge(e1_t, e)

            def e1_y_lo(e, prev):
                dve.wait_ge(e1_yhi, e + 1)
                nc.vector.tensor_tensor(yb[:, prev, :, C:], ps_y[:, :, :C], yb[:, prev, :, :C].bitcast(f32),
                                        ALU.subtract).then_inc(y2_ready, 1)

            def row1(s, row, o, quads, t, first):
                m = 0
                for q in quads:
                    for k in ks(1, q):
                        if first:
                            ln_first(m, k)
                            split(t, m)
                            if m:
                                dve.wait_ge(y1_ready, m)
                            ln_second(m)
                            dve.wait_ge(y1_hi, m + 1)
                            nc.vector.tensor_tensor(ya[:, k, :, C:], hs[:, :, :], ya[:, k, :, :C].bitcast(f32),
                                                    ALU.subtract).then_inc(y1_ready, 1)
                        else:
                            if m == 2:
                                e1_take(o - 1, row - 1, t)
                            if m == 3:
                                e1_norm(o - 1, row - 1)
                            if m == 4:
                                e1_hs_free(o - 1)
                                ln_second(NB + o - 1)
                            if m == 6:
                                e1_y_lo(o - 1, row - 1)
                            split(t, m)
                        m += 1

            dve.wait_ge(x_in, 16)
            over_rows(dve, 1, row1)
            e1_take(NB - 1, NB - 1, T2)
            dve.wait_ge(e1_mt, NB)
            nc.vector.memset(acc_a[:, :, :], 0.0).then_inc(zeroed, 1)
            e1_norm(NB - 1, NB - 1)
            e1_hs_free(NB - 1)
            ln_second(2 * NB - 1)
            e1_y_lo(NB - 1, NB - 1)

            G_STEPS = 5

            def g_take(e, prev, t, acc):
                dve.wait_ge(used, t + SPL)
                nc.vector.tensor_tensor(mt[:, :], acc[:, prev % 2, :], part[:, prev, :], ALU.add).then_inc(g_mt, 1)

            def g_state(e, prev, last):
                def step(i, ins):
                    ins.then_inc(g_step, 1)
                    dve.wait_ge(g_step, e * G_STEPS + i)
                dve.wait_ge(g_rz, e + 1)
                step(1, nc.vector.tensor_tensor(sq[:, :, :], rz[:, :, :C], ps_g[:, :, 3 * C:], ALU.mult))
                nc.vector.tensor_tensor(sq[:, :, :], sq[:, :, :], ps_g[:, :, 2 * C:3 * C], ALU.add).then_inc(g_narg, 1)
                dve.wait_ge(g_n, e + 1)
                step(2, nc.vector.tensor_tensor(dev[:, :, :], hs[:, :, :], sq[:, :, :], ALU.subtract))
                step(3, nc.vector.tensor_tensor(dev[:, :, :], dev[:, :, :], rz[:, :, C:], ALU.mult))
                step(4, nc.vector.tensor_tensor(dev[:, :, :], dev[:, :, :], sq[:, :, :], ALU.add))
                if last:
                    step(5, nc.vector.scalar_tensor_tensor(out=hs[:, :, :], in0=dev[:, :, :], scalar=0.0,
                                                           in1=x1[:, prev, :, :], op0=ALU.max, op1=ALU.add))
                    dve.sem_inc(g_h, 1)
                else:
                    step(5, nc.vector.tensor_scalar(hs[:, :, :], dev[:, :, :], 0.0, None, ALU.max))
                    dve.sem_inc(g_h, 1)

            def g_y_lo(e, prev):
                dve.wait_ge(g_yhi, e + 1)
                nc.vector.tensor_tensor(ya[:, prev, :, C:], ps_y[:, :, :C], ya[:, prev, :, :C].bitcast(f32),
                                        ALU.subtract).then_inc(y3_ready, 1)

            def gru_rows(sweep):
                acc = acc_b if sweep == 2 else acc_a

                def row(s, row_, o, quads, t, first):
                    prev = row_ + 1
                    e = o - 1 if sweep == 2 else NB + o - 1
                    for m in range(QUAD * len(quads)):
                        if not first:
                            if m == 2:
                                g_take(e, prev, t, acc)
                            if m == 3:
                                g_state(e, prev, sweep == 3)
                            if sweep == 2 and len(quads) > 1 and m == 6:
                                g_y_lo(e, prev)
                        split(t, m)
                    if sweep == 2 and len(quads) == 1 and not first:
                        g_y_lo(e, prev)
                return row

            over_rows(dve, 2, gru_rows(2))
            g_take(NB - 1, 0, T3, acc_b)
            g_state(NB - 1, 0, False)
            g_y_lo(NB - 1, 0)
            over_rows(dve, 3, gru_rows(3))
            g_take(2 * NB - 1, 0, T_END, acc_a)
            g_state(2 * NB - 1, 0, True)

        @block.gpsimd
        def _(pool):
            with pool.Fori(0, NB) as e:
                pool.wait_ge(h_ready, NB + e + 1)
                pool.sem_inc(past_pool, 1)
                nc.gpsimd.tensor_copy(hall[:, e, :, :], hs[:, :, :]).then_inc(e1_kept, 1)
            def fetch(e, row):
                nc.gpsimd.tensor_copy(hs[:, :, :], hall[:, row, :, :]).then_inc(g_old, 1)
            pool.wait_ge(e1_kept, NB)
            pool.wait_ge(e1_t, NB)
            fetch(0, NB - 1)
            with pool.Fori(0, NB - 1) as e:
                pool.wait_ge(g_h, e + 1)
                pool.sem_inc(past_pool, 1)
                nc.gpsimd.tensor_copy(hall[:, NB - 1 - e, :, :], hs[:, :, :]).then_inc(g_kept, 1)
                pool.wait_ge(g_kept, e + 1)
                pool.sem_inc(past_pool, 1)
                pool.wait_ge(g_t, e + 1)
                pool.sem_inc(past_pool, 1)
                fetch(e + 1, NB - 2 - e)
            pool.wait_ge(g_h, NB)
            nc.gpsimd.tensor_copy(hall[:, 0, :, :], hs[:, :, :]).then_inc(g_kept, 1)
            pool.wait_ge(g_kept, NB)
            pool.wait_ge(g_t, NB)
            fetch(NB, NB - 1)
            with pool.Fori(0, NB - 1) as e:
                pool.wait_ge(g_h, NB + e + 1)
                pool.sem_inc(past_pool, 1)
                pool.dma_start(out[NB - 1 - e, :, :], hs[:, :, :]).then_inc(stored, 16)
                pool.wait_ge(stored, 16 * (e + 1))
                pool.sem_inc(past_pool, 1)
                fetch(NB + e + 1, NB - 2 - e)
            pool.wait_ge(g_h, 2 * NB)
            pool.dma_start(out[0, :, :], hs[:, :, :]).then_inc(stored, 16)

        @block.tensor
        def _(pe):
            pe.sem_inc(used, SPL)
            pe.wait_ge(consts_in, 16 * 11)

            def multiply(y, k, m, acc, first, last):
                for kt in range(KT):
                    yield [(acc, y[:, k, kt, :], half[:, m % SPL, kt * B:(kt + 1) * B],
                            first and kt == 0 and half is hi, last and kt == KT - 1 and half is lo)
                           for half in (hi, lo)]

            def product(t, m, parts):
                pe.wait_ge(lo_ready, t + m + 1 + RAW)
                for kt in range(KT):
                    for y, k, acc, opens, closes in parts:
                        for half in (hi, lo):
                            last = nc.tensor.matmul(acc, y[:, k, kt, :], half[:, m % SPL, kt * B:(kt + 1) * B],
                                                    start=opens and kt == 0 and half is hi,
                                                    stop=closes and kt == KT - 1 and half is lo)
                last.then_inc(used, 1)

            def transpose_state(sem_done):
                for i in range(KT):
                    last = nc.tensor.transpose(ps_t[:C, i * P:(i + 1) * P], hs[:, i, :], ident[:, :])
                last.then_inc(sem_done, 1)

            def times(dst, lhs, rows, w, sem_done):
                for i in range(KT):
                    last = nc.tensor.matmul(dst[:, i, :C], lhs[:rows, i * P:(i + 1) * P], w[:rows, :],
                                            start=True, stop=True)
                last.then_inc(sem_done, 1)

            def e1_project(e):
                pe.wait_ge(e1_mt, e + 1)
                times(ps_y, mt, P, w0s, e1_agg)

            def e1_transpose(e):
                pe.wait_ge(h_ready, NB + e + 1)
                pe.sem_inc(past_pe, 1)
                transpose_state(e1_t)

            def e1_next(e):
                pe.wait_ge(e1_ht, e + 1)
                times(ps_y, ht, C, w1s, e1_y)

            def row1(s, row, o, quads, t, first):
                if not first:
                    pe.wait_ge(e1_mt, o - 1)
                    pe.wait_ge(e1_part, o - 1)
                m = 0
                for q in quads:
                    for k in ks(1, q):
                        parts = [(ya, k, acc_a[:, row % 2, :], m == 0, m == NB - 1)]
                        if first:
                            pe.wait_ge(y1_ready, m + 1)
                        if q < s:
                            if k == QUAD * s - 1:
                                pe.wait_ge(y2_ready, o)
                            parts.append((yb, k, acc_b[:, row % 2, :], k == QUAD * s - 1, k == 0))
                        product(t, m, parts)
                        if not first:
                            if m == 0:
                                e1_project(o - 1)
                            if m == 2:
                                e1_transpose(o - 1)
                            if m == 3:
                                e1_next(o - 1)
                        m += 1

            over_rows(pe, 1, row1)
            e1_project(NB - 1)
            e1_transpose(NB - 1)
            e1_next(NB - 1)

            def g_old_transpose(e):
                pe.wait_ge(g_old, e + 1)
                pe.sem_inc(past_pe, 1)
                transpose_state(g_oldt)

            def g_sums(e, layer):
                pe.wait_ge(g_mt, e + 1)
                pe.wait_ge(g_oldht, e + 1)
                for i in range(KT):
                    nc.tensor.matmul(ps_g[:, i, :], ht[:, i * P:(i + 1) * P], wh[layer][:, :], start=True, stop=False)
                    last = nc.tensor.matmul(ps_g[:, i, :3 * C], mt[:, i * P:(i + 1) * P], wi[layer][:, :],
                                            start=False, stop=True)
                last.then_inc(g_gates, 1)

            def g_transpose(e):
                pe.wait_ge(g_h, e + 1)
                pe.sem_inc(past_pe, 1)
                transpose_state(g_t)

            def g_next(e):
                pe.wait_ge(g_ht, e + 1)
                times(ps_y, ht, C, w2s, g_y)

            def gru_rows(sweep):
                def row(s, row_, o, quads, t, first):
                    e = o - 1 if sweep == 2 else NB + o - 1
                    if not first:
                        pe.wait_ge(g_mt, e)
                        if sweep == 2:
                            pe.wait_ge(g_part, e)
                    m = 0
                    for q in quads:
                        for k in ks(sweep, q):
                            if sweep == 2:
                                parts = [(yb, k, acc_b[:, row_ % 2, :], m == 0, m == QUAD * len(quads) - 1)]
                                if q > s:
                                    if k == QUAD * (s + 1):
                                        pe.wait_ge(y3_ready, o)
                                    parts.append((ya, k, acc_a[:, row_ % 2, :], k == QUAD * (s + 1), k == NB - 1))
                            else:
                                parts = [(ya, k, acc_a[:, row_ % 2, :], m == 0, k == 0)]
                            product(t, m, parts)
                            if not first:
                                if m == 0:
                                    g_old_transpose(e)
                                if m == 1:
                                    g_sums(e, sweep - 2)
                                if m == 2 and sweep == 2:
                                    g_transpose(e)
                                if m == 3 and sweep == 2:
                                    g_next(e)
                            m += 1
                return row

            pe.wait_ge(y2_ready, NB)
            pe.wait_ge(zeroed, 2)
            over_rows(pe, 2, gru_rows(2))
            g_old_transpose(NB - 1)
            g_sums(NB - 1, 0)
            g_transpose(NB - 1)
            g_next(NB - 1)
            pe.wait_ge(y3_ready, NB)
            pe.wait_ge(g_part, NB)
            over_rows(pe, 3, gru_rows(3))
            g_old_transpose(2 * NB - 1)
            g_sums(2 * NB - 1, 1)


def kernel(x, adj, L0_gnn_weight, L1_gnn_W1, L1_gnn_wih1, L1_gnn_whh1, L1_gnn_bih1, L1_gnn_bhh1,
           L1_gnn_W2, L1_gnn_wih2, L1_gnn_whh2, L1_gnn_bih2, L1_gnn_bhh2):
    import concourse.bacc as bacc
    from concourse.bass_utils import run_bass_kernel_spmd

    def lay(a):
        return np.ascontiguousarray(np.asarray(a))

    def hidden(whh, bih, bhh):
        a = np.zeros((C + 2, G), np.float32)
        whh_t = np.asarray(whh).T
        a[:C, :2 * C] = whh_t[:, :2 * C]
        a[:C, 3 * C:] = whh_t[:, 2 * C:]
        a[C, :3 * C] = np.asarray(bih)
        a[C + 1, :2 * C] = np.asarray(bhh)[:2 * C]
        a[C + 1, 3 * C:] = np.asarray(bhh)[2 * C:]
        return a

    blocks = lay(np.asarray(adj).reshape(NB, B, NB, KT, P).transpose(0, 2, 4, 3, 1)).reshape(NB, NB, P, KT * B)
    arrays = {
        "blocks": blocks,
        "x": lay(np.asarray(x).reshape(NB, KT, P, C).transpose(2, 0, 1, 3)),
        "w0": lay(L0_gnn_weight), "w1": lay(L1_gnn_W1), "w2": lay(L1_gnn_W2),
        "wi1": lay(np.asarray(L1_gnn_wih1).T), "wi2": lay(np.asarray(L1_gnn_wih2).T),
        "wh1": hidden(L1_gnn_whh1, L1_gnn_bih1, L1_gnn_bhh1),
        "wh2": hidden(L1_gnn_whh2, L1_gnn_bih2, L1_gnn_bhh2),
        "ident": np.eye(P, dtype=np.float32),
    }
    nc = bacc.Bacc("TRN2", target_bir_lowering=False, num_devices=1)
    args = [nc.dram_tensor(f"in_{n}", a.shape, mybir.dt.from_np(a.dtype), kind="ExternalInput").ap()
            for n, a in arrays.items()]
    out = nc.dram_tensor("out_x", (NB, P, KT * C), mybir.dt.float32, kind="ExternalOutput").ap()
    build(nc, *args, out)
    r = run_bass_kernel_spmd(nc, [{f"in_{n}": a for n, a in arrays.items()}], core_ids=[0])
    got = r.results[0]["out_x"]
    return got.reshape(NB, P, KT, C).transpose(0, 2, 1, 3).reshape(N, C)
```

```python
import numpy as np
import concourse.bass as bass
from concourse import mybir
from concourse.alu_op_type import AluOpType as ALU
from contextlib import ExitStack

N, C = 8192, 64
P = 128
B = 512
NB = N // B
KT = B // P
QUAD = 4
NQ = NB // QUAD
RAW = 4
UNITS = 2
UW = KT * B // UNITS
SPL = 4
EPS = 1e-5
G = 4 * C


def build(nc, blocks, x, w0, w1, w2, wi1, wi2, wh1, wh2, ident_in, out):
    f32, f32r = mybir.dt.float32, mybir.dt.float32r
    ACT = mybir.ActivationFunctionType
    AX = mybir.AxisListType
    ctx = ExitStack()
    with ctx:
        def sb(name, shape, dt=f32):
            return ctx.enter_context(nc.sbuf_tensor(name, shape, dt))

        def pb(name, shape):
            return ctx.enter_context(nc.psum_tensor(name, shape, f32))

        def sem(name):
            return ctx.enter_context(nc.semaphore(name))

        ya = sb("ya", [P, NB, KT, 2 * C], f32r)
        yb = sb("yb", [P, NB, KT, 2 * C], f32r)
        part = sb("part", [P, NB, B])
        x1 = sb("x1", [P, NB, KT, C])
        hall = sb("hall", [P, NB, KT, C])
        raw = sb("raw", [P, RAW, UNITS, UW])
        hi = sb("hi", [P, SPL, UW], f32r)
        lo = sb("lo", [P, SPL, UW], f32r)
        w0s = sb("w0s", [P, C])
        w1s = sb("w1s", [C, C])
        w2s = sb("w2s", [C, C])
        wi = [sb("wi1s", [P, 3 * C]), sb("wi2s", [P, 3 * C])]
        wh = [sb("wh1s", [C + 2, G]), sb("wh2s", [C + 2, G])]
        ident = sb("ident", [P, P])
        mt = sb("mt", [P, B])
        ht = sb("ht", [C + 2, B])
        hs = sb("hs", [P, KT, C])
        dev = sb("dev", [P, KT, C])
        sq = sb("sq", [P, KT, C])
        st = sb("st", [P, 5, KT])
        rz = sb("rz", [P, KT, 2 * C])
        acc_a = pb("acc_a", [P, 2, B])
        acc_b = pb("acc_b", [P, 2, B])
        ps_g = pb("ps_g", [P, KT, G])
        ps_t = pb("ps_t", [P, B])
        ps_y = pb("ps_y", [P, KT, P])

        loaded = [sem(f"loaded{s}") for s in range(RAW)]
        hi_ready = sem("hi_ready")
        lo_ready = sem("lo_ready")
        used = sem("used")
        consts_in = sem("consts_in")
        x_in = sem("x_in")
        zeroed = sem("zeroed")
        ones_set = sem("ones_set")
        ln_step = sem("ln_step")
        var_ready = sem("var_ready")
        std_ready = sem("std_ready")
        h_ready = sem("h_ready")
        y1_hi = sem("y1_hi")
        y1_ready = sem("y1_ready")
        e1_mt = sem("e1_mt")
        e1_part = sem("e1_part")
        e1_agg = sem("e1_agg")
        e1_x1 = sem("e1_x1")
        e1_t = sem("e1_t")
        e1_ht = sem("e1_ht")
        e1_kept = sem("e1_kept")
        e1_y = sem("e1_y")
        e1_yhi = sem("e1_yhi")
        y2_ready = sem("y2_ready")
        g_old = sem("g_old")
        g_oldt = sem("g_oldt")
        g_oldht = sem("g_oldht")
        g_mt = sem("g_mt")
        g_part = sem("g_part")
        g_gates = sem("g_gates")
        g_rz = sem("g_rz")
        g_step = sem("g_step")
        g_narg = sem("g_narg")
        g_n = sem("g_n")
        g_h = sem("g_h")
        g_t = sem("g_t")
        g_ht = sem("g_ht")
        g_kept = sem("g_kept")
        g_y = sem("g_y")
        g_yhi = sem("g_yhi")
        y3_ready = sem("y3_ready")
        stored = sem("stored")

        past_sp, past_dve, past_pool, past_pe = (sem(f"past_{e}") for e in ("sp", "dve", "pool", "pe"))

        block = ctx.enter_context(nc.Block())

        def runs(sweep):
            t0 = {1: 0, 2: NB * NB, 3: NB * NB + QUAD * QUAD * NQ * (NQ + 1) // 2}[sweep]
            found = []
            for s in (range(NQ) if sweep == 1 else range(NQ - 1, -1, -1)):
                quads = {1: list(range(NQ - 1, -1, -1)),
                         2: [s, *range(s + 2, NQ), *range(s + 1, min(s + 2, NQ))],
                         3: list(range(s, -1, -1))}[sweep]
                first, step = (QUAD * s, 1) if sweep == 1 else (QUAD * s + QUAD - 1, -1)
                cuts = [(first, QUAD)]
                if (sweep == 1 and s == 0) or (sweep > 1 and s == NQ - 1):
                    cuts = [(first, 1), (first + step, QUAD - 1)]
                for a, n in cuts:
                    found.append((s, a, step, n, quads, t0))
                    t0 += n * len(quads) * QUAD
            return found

        def ks(q):
            return range(QUAD * q + QUAD - 1, QUAD * q - 1, -1)

        def gru_turns(blocks_of_row):
            if blocks_of_row == QUAD:
                return {"old": 0, "take": 2, "sums": 1, "sigmoid": 3, "tanh": 3, "turn": 2, "turned": 4, "y": 3, "y_halves": 4}
            return {"old": 0, "take": 2, "sums": 1, "sigmoid": 4, "tanh": 5, "turn": 3, "turned": 6, "y": 4, "y_halves": 7}

        T2 = NB * NB
        T3 = T2 + QUAD * QUAD * NQ * (NQ + 1) // 2
        T_END = 2 * T3 - T2

        def over_rows(eng, sweep, body):
            for s, a, step, n, quads, t0 in runs(sweep):
                o = a if sweep == 1 else NB - 1 - a
                if n == 1:
                    body(s, a, o, quads, t0, True)
                else:
                    with eng.Fori(0, n) as r:
                        body(s, a + step * r, o + r, quads, t0 + r * (QUAD * len(quads)), False)

        @block.sync
        def _(sp):
            def load(row, k, t, m):
                sp.wait_ge(lo_ready, UNITS * (t + m + 1))
                sp.sem_inc(past_sp, 1)
                sp.dma_start(raw[:, m % RAW, :, :].rearrange("p u w -> p (u w)"), blocks[row, k, :, :]).then_inc(loaded[m % RAW], 16)

            for sweep in (1, 2, 3):
                def row_loads(s, row, o, quads, t, first):
                    m = 0
                    for q in quads:
                        for k in ks(q):
                            load(row, k, t, m)
                            m += 1
                over_rows(sp, sweep, row_loads)
            sp.wait_ge(stored, 16 * NB)

        @block.scalar
        def _(act):
            act.dma_start(x1[:, :, :, :], x).then_inc(x_in, 16)
            for dst, src in ((w0s[:C, :], w0), (w0s[C:, :], w0), (w1s[:, :], w1), (w2s[:, :], w2),
                             (wi[0][:C, :], wi1), (wi[0][C:, :], wi1), (wi[1][:C, :], wi2), (wi[1][C:, :], wi2),
                             (wh[0][:, :], wh1), (wh[1][:, :], wh2), (ident[:, :], ident_in)):
                act.dma_start(dst, src).then_inc(consts_in, 16)

            def split(t, m):
                act.wait_ge(loaded[m % RAW], (t + m - m % RAW) * (16 // RAW) + 16)
                for u in range(UNITS):
                    slot = (UNITS * m + u) % SPL
                    act.wait_ge(used, UNITS * (t + m) + u + 1)
                    nc.scalar.copy(hi[:, slot, :], raw[:, m % RAW, u, :]).then_inc(hi_ready, 1)

            def root(e):
                act.wait_ge(var_ready, e + 1)
                nc.scalar.activation(st[:, 3, :], st[:, 2, :], ACT.Sqrt).then_inc(std_ready, 1)

            def transposed(src_sem, n, dst_sem):
                act.wait_ge(src_sem, n)
                nc.scalar.copy(ht[:C, :], ps_t[:C, :]).then_inc(dst_sem, 1)

            def row1(s, row, o, quads, t, first):
                m = 0
                for q in quads:
                    for k in ks(q):
                        if first:
                            split(t, m)
                            root(m)
                            act.wait_ge(h_ready, m + 1)
                            nc.scalar.copy(ya[:, k, :, :C], hs[:, :, :]).then_inc(y1_hi, 1)
                        else:
                            if m == 2:
                                e1_part_save(o - 1, row - 1, t)
                            if m == 4:
                                root(NB + o - 1)
                            if m == 5:
                                transposed(e1_t, o, e1_ht)
                            if m == 6:
                                e1_y_hi(o - 1, row - 1)
                            split(t, m)
                        m += 1

            def e1_part_save(e, prev, t):
                act.wait_ge(used, UNITS * t + SPL)
                nc.scalar.copy(part[:, prev, :], acc_b[:, prev % 2, :]).then_inc(e1_part, 1)

            def e1_y_hi(e, prev):
                act.wait_ge(e1_y, e + 1)
                nc.scalar.copy(yb[:, prev, :, :C], ps_y[:, :, :C]).then_inc(e1_yhi, 1)

            act.wait_ge(zeroed, 1)
            over_rows(act, 1, row1)
            e1_part_save(NB - 1, NB - 1, T2)
            root(2 * NB - 1)
            transposed(e1_t, NB, e1_ht)
            e1_y_hi(NB - 1, NB - 1)

            def g_sig(e):
                act.wait_ge(g_gates, e + 1)
                nc.scalar.activation(rz[:, :, :], ps_g[:, :, :2 * C], ACT.Sigmoid).then_inc(g_rz, 1)

            def g_tanh(e):
                act.wait_ge(g_narg, e + 1)
                nc.scalar.activation(sq[:, :, :], sq[:, :, :], ACT.Tanh).then_inc(g_n, 1)

            def g_part_save(e, prev, t):
                act.wait_ge(g_mt, e + 1)
                nc.scalar.copy(part[:, prev, :], acc_a[:, prev % 2, :]).then_inc(g_part, 1)

            def g_y_hi(e, prev):
                act.wait_ge(g_y, e + 1)
                nc.scalar.copy(ya[:, prev, :, :C], ps_y[:, :, :C]).then_inc(g_yhi, 1)

            def gru_rows(sweep):
                def row(s, row_, o, quads, t, first):
                    ends = 2 if first else sweep
                    prev, e = (0, NB - 1) if first else (row_ + 1, o - 1 + NB * (sweep - 2))
                    turn = gru_turns(QUAD * len(quads))
                    for m in range(QUAD * len(quads) + 1):
                        if not (first and sweep == 2):
                            if m == turn["take"]:
                                transposed(g_oldt, e + 1, g_oldht)
                                if ends == 2:
                                    g_part_save(e, prev, t)
                            if m == turn["sigmoid"]:
                                g_sig(e)
                            if m == turn["tanh"]:
                                g_tanh(e)
                            if ends == 2 and m == turn["turned"]:
                                transposed(g_t, e + 1, g_ht)
                            if ends == 2 and m == turn["y_halves"]:
                                g_y_hi(e, prev)
                        if m < QUAD * len(quads):
                            split(t, m)
                return row

            act.wait_ge(zeroed, 2)
            over_rows(act, 2, gru_rows(2))
            over_rows(act, 3, gru_rows(3))
            transposed(g_oldt, 2 * NB, g_oldht)
            g_sig(2 * NB - 1)
            g_tanh(2 * NB - 1)

        @block.vector
        def _(dve):
            dve.sem_inc(lo_ready, UNITS * RAW)
            nc.vector.memset(acc_b[:, :, :], 0.0).then_inc(zeroed, 1)
            nc.vector.memset(ht[C:, :], 1.0).then_inc(ones_set, 1)

            def split(t, m):
                for u in range(UNITS):
                    slot = (UNITS * m + u) % SPL
                    dve.wait_ge(hi_ready, UNITS * (t + m) + u + 1)
                    nc.vector.tensor_tensor(lo[:, slot, :], raw[:, m % RAW, u, :], hi[:, slot, :].bitcast(f32),
                                            ALU.subtract).then_inc(lo_ready, 1)

            LN_STEPS = 6

            def ln_first(e, row):
                def step(i, ins):
                    ins.then_inc(ln_step, 1)
                    dve.wait_ge(ln_step, e * LN_STEPS + i)
                step(1, nc.vector.tensor_reduce(st[:, 0, :], x1[:, row, :, :], AX.X, ALU.add))
                step(2, nc.vector.tensor_scalar(st[:, 1, :], st[:, 0, :], -1.0 / C, None, ALU.mult))
                step(3, nc.vector.tensor_tensor(dev[:, :, :], x1[:, row, :, :],
                                                st[:, 1, :].unsqueeze(2).to_broadcast([P, KT, C]), ALU.add))
                step(4, nc.vector.tensor_tensor(sq[:, :, :], dev[:, :, :], dev[:, :, :], ALU.mult))
                step(5, nc.vector.tensor_reduce(st[:, 0, :], sq[:, :, :], AX.X, ALU.add))
                nc.vector.tensor_scalar(st[:, 2, :], st[:, 0, :], 1.0 / C, EPS, ALU.mult, ALU.add).then_inc(var_ready, 1)

            def ln_second(e):
                dve.wait_ge(std_ready, e + 1)
                nc.vector.reciprocal(st[:, 4, :], st[:, 3, :]).then_inc(ln_step, 1)
                dve.wait_ge(ln_step, e * LN_STEPS + 6)
                nc.vector.scalar_tensor_tensor(out=hs[:, :, :], in0=dev[:, :, :], scalar=0.0,
                                               in1=st[:, 4, :].unsqueeze(2).to_broadcast([P, KT, C]),
                                               op0=ALU.max, op1=ALU.mult).then_inc(h_ready, 1)

            def e1_take(e, prev, t):
                dve.wait_ge(used, UNITS * t + SPL)
                nc.vector.tensor_copy(mt[:, :], acc_a[:, prev % 2, :]).then_inc(e1_mt, 1)

            def e1_norm(e, prev):
                dve.wait_ge(e1_agg, e + 1)
                nc.vector.tensor_tensor(x1[:, prev, :, :], x1[:, prev, :, :], ps_y[:, :, :C], ALU.add)\
                    .then_inc(e1_x1, 1)
                dve.wait_ge(e1_x1, e + 1)
                dve.sem_inc(past_dve, 1)
                ln_first(NB + e, prev)

            def e1_y_lo(e, prev):
                dve.wait_ge(e1_kept, e + 1)
                dve.wait_ge(e1_yhi, e + 1)
                nc.vector.tensor_tensor(yb[:, prev, :, C:], ps_y[:, :, :C], yb[:, prev, :, :C].bitcast(f32),
                                        ALU.subtract).then_inc(y2_ready, 1)

            def row1(s, row, o, quads, t, first):
                m = 0
                for q in quads:
                    for k in ks(q):
                        if first:
                            ln_first(m, k)
                            split(t, m)
                            if m:
                                dve.wait_ge(y1_ready, m)
                            ln_second(m)
                            dve.wait_ge(y1_hi, m + 1)
                            nc.vector.tensor_tensor(ya[:, k, :, C:], hs[:, :, :], ya[:, k, :, :C].bitcast(f32),
                                                    ALU.subtract).then_inc(y1_ready, 1)
                        else:
                            if m == 2:
                                e1_take(o - 1, row - 1, t)
                            if m == 3:
                                e1_norm(o - 1, row - 1)
                            if m == 4:
                                ln_second(NB + o - 1)
                            if m == 6:
                                e1_y_lo(o - 1, row - 1)
                            split(t, m)
                        m += 1

            dve.wait_ge(x_in, 16)
            over_rows(dve, 1, row1)
            e1_take(NB - 1, NB - 1, T2)
            dve.wait_ge(e1_mt, NB)
            nc.vector.memset(acc_a[:, :, :], 0.0).then_inc(zeroed, 1)
            e1_norm(NB - 1, NB - 1)
            ln_second(2 * NB - 1)
            e1_y_lo(NB - 1, NB - 1)

            G_STEPS = 5

            def g_do(e, i, ins):
                ins.then_inc(g_step, 1)
                dve.wait_ge(g_step, e * G_STEPS + i)

            def g_take(e, prev, t, acc):
                dve.wait_ge(used, UNITS * t + SPL)
                nc.vector.tensor_tensor(mt[:, :], acc[:, prev % 2, :], part[:, prev, :], ALU.add).then_inc(g_mt, 1)

            def g_argument(e):
                dve.wait_ge(g_rz, e + 1)
                g_do(e, 1, nc.vector.tensor_tensor(sq[:, :, :], rz[:, :, :C], ps_g[:, :, 3 * C:], ALU.mult))
                nc.vector.tensor_tensor(sq[:, :, :], sq[:, :, :], ps_g[:, :, 2 * C:3 * C], ALU.add).then_inc(g_narg, 1)

            def g_state(e, prev, last):
                def step(i, ins):
                    g_do(e, i, ins)
                dve.wait_ge(g_n, e + 1)
                step(2, nc.vector.tensor_tensor(dev[:, :, :], hs[:, :, :], sq[:, :, :], ALU.subtract))
                step(3, nc.vector.tensor_tensor(dev[:, :, :], dev[:, :, :], rz[:, :, C:], ALU.mult))
                step(4, nc.vector.tensor_tensor(dev[:, :, :], dev[:, :, :], sq[:, :, :], ALU.add))
                if last:
                    step(5, nc.vector.scalar_tensor_tensor(out=hs[:, :, :], in0=dev[:, :, :], scalar=0.0,
                                                           in1=x1[:, prev, :, :], op0=ALU.max, op1=ALU.add))
                    dve.sem_inc(g_h, 1)
                else:
                    step(5, nc.vector.tensor_scalar(hs[:, :, :], dev[:, :, :], 0.0, None, ALU.max))
                    dve.sem_inc(g_h, 1)

            def g_y_lo(e, prev):
                dve.wait_ge(g_yhi, e + 1)
                nc.vector.tensor_tensor(ya[:, prev, :, C:], ps_y[:, :, :C], ya[:, prev, :, :C].bitcast(f32),
                                        ALU.subtract).then_inc(y3_ready, 1)

            def gru_rows(sweep):
                def row(s, row_, o, quads, t, first):
                    ends = 2 if first else sweep
                    prev, e = (0, NB - 1) if first else (row_ + 1, o - 1 + NB * (sweep - 2))
                    turn = gru_turns(QUAD * len(quads))
                    for m in range(QUAD * len(quads) + 1):
                        if not (first and sweep == 2):
                            if m == turn["take"]:
                                g_take(e, prev, t, acc_b if ends == 2 else acc_a)
                            if m == turn["sigmoid"]:
                                g_argument(e)
                            if m == turn["tanh"]:
                                g_state(e, prev, ends == 3)
                            if ends == 2 and m == turn["y_halves"]:
                                g_y_lo(e, prev)
                        if m < QUAD * len(quads):
                            split(t, m)
                return row

            over_rows(dve, 2, gru_rows(2))
            over_rows(dve, 3, gru_rows(3))
            g_take(2 * NB - 1, 0, T_END, acc_a)
            g_argument(2 * NB - 1)
            g_state(2 * NB - 1, 0, True)

        @block.gpsimd
        def _(pool):
            with pool.Fori(0, NB) as e:
                pool.wait_ge(h_ready, NB + e + 1)
                pool.sem_inc(past_pool, 1)
                nc.gpsimd.tensor_copy(hall[:, e, :, :], hs[:, :, :]).then_inc(e1_kept, 1)
            def fetch(e, row):
                nc.gpsimd.tensor_copy(hs[:, :, :], hall[:, row, :, :]).then_inc(g_old, 1)
            pool.wait_ge(e1_kept, NB)
            pool.wait_ge(e1_t, NB)
            fetch(0, NB - 1)
            with pool.Fori(0, NB - 1) as e:
                pool.wait_ge(g_h, e + 1)
                pool.sem_inc(past_pool, 1)
                nc.gpsimd.tensor_copy(hall[:, NB - 1 - e, :, :], hs[:, :, :]).then_inc(g_kept, 1)
                pool.wait_ge(g_kept, e + 1)
                pool.sem_inc(past_pool, 1)
                pool.wait_ge(g_t, e + 1)
                pool.sem_inc(past_pool, 1)
                fetch(e + 1, NB - 2 - e)
            pool.wait_ge(g_h, NB)
            nc.gpsimd.tensor_copy(hall[:, 0, :, :], hs[:, :, :]).then_inc(g_kept, 1)
            pool.wait_ge(g_kept, NB)
            pool.wait_ge(g_t, NB)
            fetch(NB, NB - 1)
            with pool.Fori(0, NB - 1) as e:
                pool.wait_ge(g_h, NB + e + 1)
                pool.sem_inc(past_pool, 1)
                pool.dma_start(out[NB - 1 - e, :, :], hs[:, :, :]).then_inc(stored, 16)
                pool.wait_ge(stored, 16 * (e + 1))
                pool.sem_inc(past_pool, 1)
                fetch(NB + e + 1, NB - 2 - e)
            pool.wait_ge(g_h, 2 * NB)
            pool.dma_start(out[0, :, :], hs[:, :, :]).then_inc(stored, 16)

        @block.tensor
        def _(pe):
            pe.sem_inc(used, SPL)
            pe.wait_ge(consts_in, 16 * 11)

            def product(t, m, parts):
                for u in range(UNITS):
                    slot = (UNITS * m + u) % SPL
                    pe.wait_ge(lo_ready, UNITS * (t + m + RAW) + u + 1)
                    for i in range(KT // UNITS):
                        kt = KT // UNITS * u + i
                        for y, k, acc, opens, closes in parts:
                            for half in (hi, lo):
                                last = nc.tensor.matmul(acc, y[:, k, kt, :], half[:, slot, i * B:(i + 1) * B],
                                                        start=opens and kt == 0 and half is hi,
                                                        stop=closes and kt == KT - 1 and half is lo)
                    last.then_inc(used, 1)

            def transpose_state(sem_done):
                for i in range(KT):
                    last = nc.tensor.transpose(ps_t[:C, i * P:(i + 1) * P], hs[:, i, :], ident[:, :])
                last.then_inc(sem_done, 1)

            def times(dst, lhs, rows, w, sem_done):
                for i in range(KT):
                    last = nc.tensor.matmul(dst[:, i, :C], lhs[:rows, i * P:(i + 1) * P], w[:rows, :],
                                            start=True, stop=True)
                last.then_inc(sem_done, 1)

            def e1_project(e):
                pe.wait_ge(e1_mt, e + 1)
                times(ps_y, mt, P, w0s, e1_agg)

            def e1_transpose(e):
                pe.wait_ge(h_ready, NB + e + 1)
                pe.sem_inc(past_pe, 1)
                transpose_state(e1_t)

            def e1_next(e):
                pe.wait_ge(e1_ht, e + 1)
                times(ps_y, ht, C, w1s, e1_y)

            def row1(s, row, o, quads, t, first):
                if s:
                    pe.wait_ge(e1_part, o - 1)
                m = 0
                for q in quads:
                    for k in ks(q):
                        parts = [(ya, k, acc_a[:, row % 2, :], m == 0, m == NB - 1)]
                        if first:
                            pe.wait_ge(y1_ready, m + 1)
                        if q < s:
                            if k == QUAD * s - 1:
                                pe.wait_ge(y2_ready, o)
                            parts.append((yb, k, acc_b[:, row % 2, :], k == QUAD * s - 1, k == 0))
                        product(t, m, parts)
                        if not first:
                            if m == 0:
                                e1_project(o - 1)
                            if m == 2:
                                e1_transpose(o - 1)
                            if m == 3:
                                e1_next(o - 1)
                        m += 1

            over_rows(pe, 1, row1)
            e1_project(NB - 1)
            e1_transpose(NB - 1)
            e1_next(NB - 1)

            def g_old_transpose(e):
                pe.wait_ge(g_old, e + 1)
                pe.sem_inc(past_pe, 1)
                transpose_state(g_oldt)

            def g_sums(e, layer):
                pe.wait_ge(g_mt, e + 1)
                pe.wait_ge(g_oldht, e + 1)
                for i in range(KT):
                    nc.tensor.matmul(ps_g[:, i, :], ht[:, i * P:(i + 1) * P], wh[layer][:, :], start=True, stop=False)
                    last = nc.tensor.matmul(ps_g[:, i, :3 * C], mt[:, i * P:(i + 1) * P], wi[layer][:, :],
                                            start=False, stop=True)
                last.then_inc(g_gates, 1)

            def g_transpose(e):
                pe.wait_ge(g_h, e + 1)
                pe.sem_inc(past_pe, 1)
                transpose_state(g_t)

            def g_next(e):
                pe.wait_ge(g_ht, e + 1)
                times(ps_y, ht, C, w2s, g_y)

            def gru_rows(sweep):
                def row(s, row_, o, quads, t, first):
                    ends = 2 if first else sweep
                    e = NB - 1 if first else o - 1 + NB * (sweep - 2)
                    turn = gru_turns(QUAD * len(quads))
                    if sweep == 2 and len(quads) > 1:
                        pe.wait_ge(g_part, e)
                    if sweep == 3 and s == NQ - 1:
                        pe.wait_ge(g_part, NB - 1 if first else NB)
                    m = 0
                    for q in quads:
                        for k in ks(q):
                            if sweep == 2:
                                parts = [(yb, k, acc_b[:, row_ % 2, :], m == 0, m == QUAD * len(quads) - 1)]
                                if q > s:
                                    if k == QUAD * (s + 1):
                                        pe.wait_ge(y3_ready, o)
                                    parts.append((ya, k, acc_a[:, row_ % 2, :], m == QUAD, k == QUAD * (s + 1)))
                            else:
                                if first and k == 0:
                                    pe.wait_ge(y3_ready, NB)
                                parts = [(ya, k, acc_a[:, row_ % 2, :], m == 0, k == 0)]
                            product(t, m, parts)
                            if not (first and sweep == 2):
                                if m == turn["old"]:
                                    g_old_transpose(e)
                                if m == turn["sums"]:
                                    g_sums(e, ends - 2)
                                if m == turn["turn"] and ends == 2:
                                    g_transpose(e)
                                if m == turn["y"] and ends == 2:
                                    g_next(e)
                            m += 1
                return row

            pe.wait_ge(y2_ready, NB)
            pe.wait_ge(zeroed, 2)
            over_rows(pe, 2, gru_rows(2))
            over_rows(pe, 3, gru_rows(3))
            g_old_transpose(2 * NB - 1)
            g_sums(2 * NB - 1, 1)


def kernel(x, adj, L0_gnn_weight, L1_gnn_W1, L1_gnn_wih1, L1_gnn_whh1, L1_gnn_bih1, L1_gnn_bhh1,
           L1_gnn_W2, L1_gnn_wih2, L1_gnn_whh2, L1_gnn_bih2, L1_gnn_bhh2):
    import concourse.bacc as bacc
    from concourse.bass_utils import run_bass_kernel_spmd

    def lay(a):
        return np.ascontiguousarray(np.asarray(a))

    def hidden(whh, bih, bhh):
        a = np.zeros((C + 2, G), np.float32)
        whh_t = np.asarray(whh).T
        a[:C, :2 * C] = whh_t[:, :2 * C]
        a[:C, 3 * C:] = whh_t[:, 2 * C:]
        a[C, :3 * C] = np.asarray(bih)
        a[C + 1, :2 * C] = np.asarray(bhh)[:2 * C]
        a[C + 1, 3 * C:] = np.asarray(bhh)[2 * C:]
        return a

    blocks = lay(np.asarray(adj).reshape(NB, B, NB, KT, P).transpose(0, 2, 4, 3, 1)).reshape(NB, NB, P, KT * B)
    arrays = {
        "blocks": blocks,
        "x": lay(np.asarray(x).reshape(NB, KT, P, C).transpose(2, 0, 1, 3)),
        "w0": lay(L0_gnn_weight), "w1": lay(L1_gnn_W1), "w2": lay(L1_gnn_W2),
        "wi1": lay(np.asarray(L1_gnn_wih1).T), "wi2": lay(np.asarray(L1_gnn_wih2).T),
        "wh1": hidden(L1_gnn_whh1, L1_gnn_bih1, L1_gnn_bhh1),
        "wh2": hidden(L1_gnn_whh2, L1_gnn_bih2, L1_gnn_bhh2),
        "ident": np.eye(P, dtype=np.float32),
    }
    nc = bacc.Bacc("TRN2", target_bir_lowering=False, num_devices=1)
    args = [nc.dram_tensor(f"in_{n}", a.shape, mybir.dt.from_np(a.dtype), kind="ExternalInput").ap()
            for n, a in arrays.items()]
    out = nc.dram_tensor("out_x", (NB, P, KT * C), mybir.dt.float32, kind="ExternalOutput").ap()
    build(nc, *args, out)
    r = run_bass_kernel_spmd(nc, [{f"in_{n}": a for n, a in arrays.items()}], core_ids=[0])
    got = r.results[0]["out_x"]
    return got.reshape(NB, P, KT, C).transpose(0, 2, 1, 3).reshape(N, C)
```

```python
import numpy as np
import concourse.bass as bass
from concourse import mybir
from concourse.alu_op_type import AluOpType as ALU
from contextlib import ExitStack

N, C = 8192, 64
P = 128
B = 512
NB = N // B
KT = B // P
BATCH = 4
BATCHES = NB // BATCH
RAW = 4
UNITS = 2
UW = KT * B // UNITS
SPL = 4
EPS = 1e-5
G = 4 * C


E1_TURNS = {"take": 2, "project": 1, "norm": 4, "root": 5, "h": 6, "turn": 5, "turned": 8, "y": 7, "y_halves": 10}
E1_LAST = {"take": 2, "project": 1, "norm": 3, "root": 4, "h": 4, "turn": 3, "turned": 5, "y": 4, "y_halves": 6}
G_TURNS = [
    {"old": 0, "take": 2, "sums": 1, "sigmoid": 3, "tanh": 4, "turn": 3, "turned": 5, "y": 4, "y_halves": 6},
    {"old": 0, "take": 2, "sums": 1, "sigmoid": 4, "tanh": 5, "turn": 4, "turned": 6, "y": 5, "y_halves": 7},
    {"old": 0, "take": 2, "sums": 1, "sigmoid": 4, "tanh": 5, "turn": 5, "turned": 7, "y": 6, "y_halves": 9},
]
Y1_TURNS = {"mean": -5, "square": -3, "var": -2, "root": -1, "h": -1, "hi": 0}
SPAN = 5
DEFER = (14, 13, 12)
DIAGONAL = {15: 5, 14: 4, 13: 2, 12: 1}
SPARE = (0.2, 1.6)
KEEP = 5


def mixed(some, others):
    at = [(i / len(some), 1, x) for i, x in enumerate(some)] + [(i / len(others), 0, x) for i, x in enumerate(others)]
    return [x for _, _, x in sorted(at, key=lambda y: y[:2])]


def plan():
    visits = []

    def visit(sweep, row, blocks):
        t0 = visits[-1][2] + len(visits[-1][3]) if visits else 0
        uses = [(product, own, r if not own else row) for r, _, todo in blocks for product, own in todo]
        done = 0
        marked = []
        for r, k, todo in blocks:
            marks = []
            for product, own in todo:
                use = uses[done]
                marks.append((product, own, use not in uses[:done], use not in uses[done + 1:]))
                done += 1
            marked.append((r, k, marks))
        blocks = marked
        begin = t0 + len(blocks)
        if visits:
            begin = max(begin, visits[-1][4] + SPAN)
        visits.append((sweep, row, t0, blocks, begin))

    visit(1, 0, [(0, k, [(1, True)]) for k in range(NB - 1, -1, -1)])
    for row in range(1, NB):
        two = [(row, k, [(1, True), (2, True)]) for k in range(row - 1)]
        one = [(row, k, [(1, True)]) for k in range(row, NB)]
        visit(1, row, (mixed(two, one) if two else one) + [(row, row - 1, [(1, True), (2, True)])])

    left = [list(range(row + 1 + (row in DEFER))) for row in range(NB)]
    diagonals = iter(range(NB - 1 - len(DIAGONAL), -1, -1))
    for row in range(NB - 1, -1, -1):
        aside = [(r, r, [(2, False)]) for _, r in zip(range(DIAGONAL.get(row, 0)), diagonals)]
        spare = round(SPARE[0] * (NB - 1 - row) + SPARE[1]) if row not in DIAGONAL else 4
        while spare > 0:
            known = [[k for k in left[r] if k >= row + 2] for r in range(NB)]
            sizes = [(min(len(known[r]), len(left[r]) - KEEP, spare, 4), len(left[r]), r) for r in range(NB)]
            sizes = [x for x in sizes if x[0] > 0 and (x[2], 3) not in [(r, p) for r, _, ((p, _),) in aside]]
            if not sizes:
                break
            size, _, r = max(sizes, key=lambda x: (x[0] if row in DIAGONAL else 0, x[1]))
            for k in known[r][-size:]:
                aside.append((r, k, [(3, False)]))
                left[r].remove(k)
            spare -= size
        own = [(row, k, [(2, True)] + [(3, True)] * (k not in left[row])) for k in range(NB - 1, row, -1)]
        diagonal = [(row, row, [(2, True)])] if row in DIAGONAL else []
        if row == NB - 1:
            visit(2, row, aside + diagonal)
        else:
            last = own[-1:] if row not in DEFER else diagonal
            rest = own[:-1] if row not in DEFER else own
            others = aside + (diagonal if row not in DEFER else [])
            visit(2, row, (mixed(rest, others) if rest else others) + last)

    long = sorted((r for r in range(NB) if len(left[r]) >= KEEP), key=lambda r: -len(left[r]))
    short = [r for r in range(NB) if len(left[r]) < KEEP]
    order = []
    while long or short:
        order += long[:1] + short[:1]
        long, short = long[1:], short[1:]
    for row in order:
        visit(3, row, [(row, k, [(3, True)]) for k in reversed(left[row])])
    return visits, visits[-1][2] + len(visits[-1][3])


def has_p3(row):
    return row < NB - 1 and not (row == NB - 2 and row in DEFER)


def asides(visits):
    found = []
    for _, _, t0, blocks, _ in visits:
        for t, (row, _, todo) in enumerate(blocks, t0):
            for product, own, _, closes in todo:
                if not own and closes:
                    found.append((t, len(found), row, product))
    return found


def build(nc, blocks, x, w0, w1, w2, wi1, wi2, wh1, wh2, ident_in, out):
    f32, f32r = mybir.dt.float32, mybir.dt.float32r
    ACT = mybir.ActivationFunctionType
    AX = mybir.AxisListType
    ctx = ExitStack()
    with ctx:
        def sb(name, shape, dt=f32):
            return ctx.enter_context(nc.sbuf_tensor(name, shape, dt))

        def pb(name, shape):
            return ctx.enter_context(nc.psum_tensor(name, shape, f32))

        def sem(name):
            return ctx.enter_context(nc.semaphore(name))

        ya = sb("ya", [P, NB, KT, 2 * C], f32r)
        yb = sb("yb", [P, NB, KT, 2 * C], f32r)
        part = sb("part", [P, NB, B])
        x1 = sb("x1", [P, NB, KT, C])
        hall = sb("hall", [P, NB, KT, C])
        raw = sb("raw", [P, RAW, UNITS, UW])
        hi = sb("hi", [P, SPL, UW], f32r)
        lo = sb("lo", [P, SPL, UW], f32r)
        w0s = sb("w0s", [P, C])
        w1s = sb("w1s", [C, C])
        w2s = sb("w2s", [C, C])
        wi = [sb("wi1s", [P, 3 * C]), sb("wi2s", [P, 3 * C])]
        wh = [sb("wh1s", [C + 2, G]), sb("wh2s", [C + 2, G])]
        ident = sb("ident", [P, P])
        mt = sb("mt", [P, B])
        ht = sb("ht", [C + 2, B])
        hs = sb("hs", [P, KT, C])
        dev = sb("dev", [P, KT, C])
        sq = sb("sq", [P, KT, C])
        st = sb("st", [P, 5, KT])
        rz = sb("rz", [P, KT, 2 * C])
        acc_a = pb("acc_a", [P, 2, B])
        acc_b = pb("acc_b", [P, 2, B])
        ps_g = pb("ps_g", [P, KT, G])
        ps_t = ps_g[:, :B // G, :].rearrange("p a b -> p (a b)")
        acc_c = pb("acc_c", [P, B])
        ps_y = pb("ps_y", [P, KT, P])
        ACC3 = [acc_b[:, 0, :], acc_a[:, 1, :], acc_b[:, 1, :], acc_a[:, 0, :]]

        ROWS = BATCH * KT

        def rows_of(buf, b):
            first = BATCH * (BATCHES - 1 - b)
            return buf[:, first:first + BATCH, :, :].rearrange("p a k c -> p (a k) c")

        def scratch(b, i):
            first = BATCH * (BATCHES - 1 - b) + i * BATCH // 2
            return part[:, first:first + BATCH // 2, :].rearrange("p a (k c) -> p (a k) c", c=C)

        def stat(b, i):
            return rz[:, b, i * ROWS:(i + 1) * ROWS]

        def spread(per_row):
            return per_row.unsqueeze(2).to_broadcast([P, ROWS, C])

        loaded = [sem(f"loaded{s}") for s in range(RAW)]
        hi_ready = sem("hi_ready")
        lo_ready = sem("lo_ready")
        used = sem("used")
        consts_in = sem("consts_in")
        x_in = [sem("x_in_right"), sem("x_in_rest")]
        ones_set = sem("ones_set")
        y1_mean = sem("y1_mean")
        y1_dev = sem("y1_dev")
        y1_sq = sem("y1_sq")
        y1_step = sem("y1_step")
        ln_step = sem("ln_step")
        var_ready = sem("var_ready")
        std_ready = sem("std_ready")
        h_ready = sem("h_ready")
        y1_hi = sem("y1_hi")
        y1_ready = sem("y1_ready")
        e1_mt = sem("e1_mt")
        e1_part = sem("e1_part")
        e1_agg = sem("e1_agg")
        e1_x1 = sem("e1_x1")
        e1_t = sem("e1_t")
        e1_ht = sem("e1_ht")
        e1_kept = sem("e1_kept")
        e1_y = sem("e1_y")
        e1_yhi = sem("e1_yhi")
        y2_ready = sem("y2_ready")
        g_old = sem("g_old")
        g_oldt = sem("g_oldt")
        g_oldht = sem("g_oldht")
        g_mt = sem("g_mt")
        g_part = sem("g_part")
        g_gates = sem("g_gates")
        g_rz = sem("g_rz")
        g_step = sem("g_step")
        g_narg = sem("g_narg")
        g_n = sem("g_n")
        g_h = sem("g_h")
        g_t = sem("g_t")
        g_ht = sem("g_ht")
        g_kept = sem("g_kept")
        g_y = sem("g_y")
        g_yhi = sem("g_yhi")
        y3_ready = sem("y3_ready")
        aside_part = sem("aside_part")
        stored = sem("stored")
        last_stored = sem("last_stored")

        past_pool = sem("past_pool")

        block = ctx.enter_context(nc.Block())

        VISITS, T_END = plan()
        T_DONE = VISITS[-1][4] + 6

        def rows(sweep):
            found = [x for x in VISITS if x[0] == sweep]
            return [(row, o, t0, blocks_) for o, (_, row, t0, blocks_, _) in enumerate(found)]

        def ending(t):
            for v, (sweep, row, t0, blocks_, begin) in enumerate(VISITS):
                if begin <= t <= begin + 12:
                    if sweep == 1:
                        turn = E1_TURNS if row < NB - 1 else E1_LAST
                    else:
                        following = len(VISITS[v + 1][3]) if v + 1 < len(VISITS) else 0
                        turn = G_TURNS[(following >= 7) + (following >= 12)] if sweep == 2 else G_TURNS[1]
                    yield sweep, row, v % NB, t0 + len(blocks_), turn, t - begin

        @block.sync
        def _(sp):
            def load(row, k, t):
                sp.wait_ge(lo_ready, UNITS * (t + 1))
                sp.dma_start(raw[:, t % RAW, :, :].rearrange("p u w -> p (u w)"), blocks[row, k, :, :])\
                    .then_inc(loaded[t % RAW], 16)

            for _, _, t0, blocks_, _ in VISITS:
                for t, (row, k, _) in enumerate(blocks_, t0):
                    if t == RAW:
                        for dst, src in ((w0s[:C, :], w0), (w0s[C:, :], w0), (w1s[:, :], w1), (w2s[:, :], w2),
                                         (wi[0][:C, :], wi1), (wi[0][C:, :], wi1), (wi[1][:C, :], wi2),
                                         (wi[1][C:, :], wi2), (wh[0][:, :], wh1), (wh[1][:, :], wh2),
                                         (ident[:, :], ident_in)):
                            sp.dma_start(dst, src).then_inc(consts_in, 16)
                    load(row, k, t)
            last = VISITS[-1][1]
            sp.wait_ge(g_h, 2 * NB)
            sp.dma_start(out[last, :, :], x1[:, last, :, :]).then_inc(last_stored, 16)
            sp.wait_ge(stored, 16 * (NB - 1))
            sp.wait_ge(last_stored, 16)

        @block.scalar
        def _(act):
            act.dma_start(x1[:, NB - BATCH:, :, :], x[:, NB - BATCH:, :, :]).then_inc(x_in[0], 16)
            act.dma_start(x1[:, :NB - BATCH, :, :], x[:, :NB - BATCH, :, :]).then_inc(x_in[1], 16)

            def split(t):
                act.wait_ge(loaded[t % RAW], 16 * (t // RAW + 1))
                for u in range(UNITS):
                    slot = (UNITS * t + u) % SPL
                    act.wait_ge(used, UNITS * t + u + 1)
                    nc.scalar.copy(hi[:, slot, :], raw[:, t % RAW, u, :]).then_inc(hi_ready, 1)

            def root(row):
                act.wait_ge(var_ready, BATCHES + row + 1)
                nc.scalar.activation(st[:, 3, :], st[:, 2, :], ACT.Sqrt).then_inc(std_ready, 1)

            def transposed(src_sem, n, dst_sem):
                act.wait_ge(src_sem, n)
                nc.scalar.copy(ht[:C, :], ps_t[:C, :]).then_inc(dst_sem, 1)

            def y1_square(b):
                act.wait_ge(y1_dev, b + 1)
                nc.scalar.activation(scratch(b, 1), scratch(b, 0), ACT.Square).then_inc(y1_sq, 1)

            def y1_root(b):
                act.wait_ge(var_ready, b + 1)
                nc.scalar.activation(stat(b, 3), stat(b, 2), ACT.Sqrt).then_inc(std_ready, 1)

            def y1_hi_half(b):
                act.wait_ge(h_ready, b + 1)
                nc.scalar.copy(rows_of(ya, b)[:, :, :C], rows_of(hall, b)).then_inc(y1_hi, 1)

            def e1_part_save(row, end):
                act.wait_ge(used, UNITS * end + SPL)
                nc.scalar.copy(part[:, row, :], acc_b[:, row % 2, :]).then_inc(e1_part, 1)

            def e1_y_hi(row):
                act.wait_ge(e1_y, row + 1)
                nc.scalar.copy(yb[:, row, :, :C], ps_y[:, :, :C]).then_inc(e1_yhi, 1)

            def g_sig(e):
                act.wait_ge(g_gates, e + 1)
                nc.scalar.activation(rz[:, :, :], ps_g[:, :, :2 * C], ACT.Sigmoid).then_inc(g_rz, 1)

            def g_tanh(e):
                act.wait_ge(g_narg, e + 1)
                nc.scalar.activation(sq[:, :, :], sq[:, :, :], ACT.Tanh).then_inc(g_n, 1)

            def g_part_save(e, row):
                act.wait_ge(g_mt, e + 1)
                nc.scalar.copy(part[:, row, :], acc_a[:, row % 2, :]).then_inc(g_part, 1)

            def g_y_hi(e, row):
                act.wait_ge(g_y, e + 1)
                nc.scalar.copy(ya[:, row, :, :C], ps_y[:, :, :C]).then_inc(g_yhi, 1)

            y1_square(0)
            y1_root(0)
            y1_hi_half(0)
            for t in range(T_DONE):
                for b in range(1, BATCHES):
                    if t == BATCH * b + Y1_TURNS["square"]:
                        y1_square(b)
                    if t == BATCH * b + Y1_TURNS["root"]:
                        y1_root(b)
                    if t == BATCH * b + Y1_TURNS["hi"]:
                        y1_hi_half(b)
                for sweep, row, o, end, turn, at in ending(t):
                    if sweep == 1:
                        if at == turn["take"] and row > 0:
                            e1_part_save(row, end)
                        if at == turn["root"]:
                            root(row)
                        if at == turn["turned"]:
                            transposed(e1_t, row + 1, e1_ht)
                        if at == turn["y_halves"]:
                            e1_y_hi(row)
                    else:
                        e = o + NB * (sweep - 2)
                        if at == turn["take"]:
                            transposed(g_oldt, e + 1, g_oldht)
                            if sweep == 2 and has_p3(row):
                                g_part_save(e, row)
                        if at == turn["sigmoid"]:
                            g_sig(e)
                        if at == turn["tanh"]:
                            g_tanh(e)
                        if sweep == 2 and at == turn["turned"]:
                            transposed(g_t, e + 1, g_ht)
                        if sweep == 2 and at == turn["y_halves"]:
                            g_y_hi(e, row)
                if t < T_END:
                    split(t)

        @block.vector
        def _(dve):
            dve.sem_inc(lo_ready, UNITS * RAW)
            nc.vector.memset(ht[C:, :], 1.0).then_inc(ones_set, 1)

            def split(t):
                for u in range(UNITS):
                    slot = (UNITS * t + u) % SPL
                    dve.wait_ge(hi_ready, UNITS * t + u + 1)
                    nc.vector.tensor_tensor(lo[:, slot, :], raw[:, t % RAW, u, :], hi[:, slot, :].bitcast(f32),
                                            ALU.subtract).then_inc(lo_ready, 1)

            LN_STEPS = 6

            def ln_first(row):
                def step(i, ins):
                    ins.then_inc(ln_step, 1)
                    dve.wait_ge(ln_step, row * LN_STEPS + i)
                step(1, nc.vector.tensor_reduce(st[:, 0, :], x1[:, row, :, :], AX.X, ALU.add))
                step(2, nc.vector.tensor_scalar(st[:, 1, :], st[:, 0, :], -1.0 / C, None, ALU.mult))
                step(3, nc.vector.tensor_tensor(dev[:, :, :], x1[:, row, :, :],
                                                st[:, 1, :].unsqueeze(2).to_broadcast([P, KT, C]), ALU.add))
                step(4, nc.vector.tensor_tensor(sq[:, :, :], dev[:, :, :], dev[:, :, :], ALU.mult))
                step(5, nc.vector.tensor_reduce(st[:, 0, :], sq[:, :, :], AX.X, ALU.add))
                nc.vector.tensor_scalar(st[:, 2, :], st[:, 0, :], 1.0 / C, EPS, ALU.mult, ALU.add).then_inc(var_ready, 1)

            def ln_second(row):
                dve.wait_ge(std_ready, BATCHES + row + 1)
                nc.vector.reciprocal(st[:, 4, :], st[:, 3, :]).then_inc(ln_step, 1)
                dve.wait_ge(ln_step, row * LN_STEPS + 6)
                nc.vector.scalar_tensor_tensor(out=hs[:, :, :], in0=dev[:, :, :], scalar=0.0,
                                               in1=st[:, 4, :].unsqueeze(2).to_broadcast([P, KT, C]),
                                               op0=ALU.max, op1=ALU.mult).then_inc(h_ready, 1)

            def e1_take(row, end):
                dve.wait_ge(used, UNITS * end + SPL)
                nc.vector.tensor_copy(mt[:, :], acc_a[:, row % 2, :]).then_inc(e1_mt, 1)
                if row == 0:
                    nc.vector.memset(part[:, 0, :], 0.0).then_inc(e1_part, 1)

            def e1_norm(row):
                dve.wait_ge(e1_agg, row + 1)
                nc.vector.tensor_tensor(x1[:, row, :, :], x1[:, row, :, :], ps_y[:, :, :C], ALU.add)\
                    .then_inc(e1_x1, 1)
                dve.wait_ge(e1_x1, row + 1)
                ln_first(row)

            def e1_y_lo(row):
                dve.wait_ge(e1_kept, row + 1)
                dve.wait_ge(e1_yhi, row + 1)
                nc.vector.tensor_tensor(yb[:, row, :, C:], ps_y[:, :, :C], yb[:, row, :, :C].bitcast(f32),
                                        ALU.subtract).then_inc(y2_ready, 1)

            Y1_STEPS = 3

            def y1_do(b, i, ins):
                ins.then_inc(y1_step, 1)
                dve.wait_ge(y1_step, b * Y1_STEPS + i)

            def y1_means(b):
                y1_do(b, 1, nc.vector.tensor_reduce(stat(b, 0), rows_of(x1, b), AX.X, ALU.add))
                nc.vector.tensor_scalar(stat(b, 1), stat(b, 0), -1.0 / C, None, ALU.mult).then_inc(y1_mean, 1)

            def y1_var(b):
                dve.wait_ge(y1_sq, b + 1)
                y1_do(b, 2, nc.vector.tensor_reduce(stat(b, 0), scratch(b, 1), AX.X, ALU.add))
                nc.vector.tensor_scalar(stat(b, 2), stat(b, 0), 1.0 / C, EPS, ALU.mult, ALU.add).then_inc(var_ready, 1)

            def y1_h(b):
                dve.wait_ge(std_ready, b + 1)
                y1_do(b, 3, nc.vector.reciprocal(stat(b, 4), stat(b, 3)))
                nc.vector.scalar_tensor_tensor(out=rows_of(hall, b), in0=scratch(b, 0), scalar=0.0,
                                               in1=spread(stat(b, 4)), op0=ALU.max, op1=ALU.mult).then_inc(h_ready, 1)

            G_STEPS = 5

            def g_do(e, i, ins):
                ins.then_inc(g_step, 1)
                dve.wait_ge(g_step, e * G_STEPS + i)

            def g_take(e, row, end, acc, sums):
                dve.wait_ge(used, UNITS * end + SPL)
                if sums:
                    dve.wait_ge(aside_part, sums)
                nc.vector.tensor_tensor(mt[:, :], acc, part[:, row, :], ALU.add).then_inc(g_mt, 1)
                if e < NB and not has_p3(row):
                    dve.wait_ge(g_mt, e + 1)
                    nc.vector.memset(part[:, row, :], 0.0).then_inc(g_part, 1)

            def g_argument(e):
                dve.wait_ge(g_rz, e + 1)
                g_do(e, 1, nc.vector.tensor_tensor(sq[:, :, :], rz[:, :, :C], ps_g[:, :, 3 * C:], ALU.mult))
                nc.vector.tensor_tensor(sq[:, :, :], sq[:, :, :], ps_g[:, :, 2 * C:3 * C], ALU.add).then_inc(g_narg, 1)

            def g_state(e, row, last):
                def step(i, ins):
                    g_do(e, i, ins)
                dve.wait_ge(g_n, e + 1)
                step(2, nc.vector.tensor_tensor(dev[:, :, :], hs[:, :, :], sq[:, :, :], ALU.subtract))
                step(3, nc.vector.tensor_tensor(dev[:, :, :], dev[:, :, :], rz[:, :, C:], ALU.mult))
                step(4, nc.vector.tensor_tensor(dev[:, :, :], dev[:, :, :], sq[:, :, :], ALU.add))
                if last:
                    step(5, nc.vector.scalar_tensor_tensor(out=x1[:, row, :, :], in0=dev[:, :, :], scalar=0.0,
                                                           in1=x1[:, row, :, :], op0=ALU.max, op1=ALU.add))
                    dve.sem_inc(g_h, 1)
                else:
                    step(5, nc.vector.tensor_scalar(hs[:, :, :], dev[:, :, :], 0.0, None, ALU.max))
                    dve.sem_inc(g_h, 1)

            def take_aside(n, row, product, end):
                if product == 2:
                    dve.wait_ge(e1_part, row + 1)
                else:
                    dve.wait_ge(g_part, NB - row)
                if n:
                    dve.wait_ge(aside_part, n)
                dve.wait_ge(used, UNITS * end + SPL)
                nc.vector.tensor_tensor(part[:, row, :], acc_c[:, :], part[:, row, :], ALU.add).then_inc(aside_part, 1)

            def g_y_lo(e, row):
                dve.wait_ge(g_yhi, e + 1)
                nc.vector.tensor_tensor(ya[:, row, :, C:], ps_y[:, :, :C], ya[:, row, :, :C].bitcast(f32),
                                        ALU.subtract).then_inc(y3_ready, 1)

            closed = {t + 1: (n, row, product) for t, n, row, product in asides(VISITS)}
            sums_of = {(row, product): n + 1 for n, row, product in closed.values()}

            dve.wait_ge(x_in[0], 16)
            y1_means(0)
            dve.wait_ge(y1_mean, 1)
            nc.vector.tensor_tensor(scratch(0, 0), rows_of(x1, 0), spread(stat(0, 1)), ALU.add).then_inc(y1_dev, 1)
            y1_var(0)
            y1_h(0)
            for t in range(T_DONE):
                for b in range(1, BATCHES):
                    if t == max(0, BATCH * b + Y1_TURNS["mean"]):
                        if b == 1:
                            dve.wait_ge(x_in[1], 16)
                        y1_means(b)
                    if t == BATCH * b + Y1_TURNS["var"]:
                        y1_var(b)
                    if t == BATCH * b + Y1_TURNS["h"]:
                        y1_h(b)
                for sweep, row, o, end, turn, at in ending(t):
                    if sweep == 1:
                        if at == turn["take"]:
                            e1_take(row, end)
                        if at == turn["norm"]:
                            e1_norm(row)
                        if at == turn["h"]:
                            ln_second(row)
                        if at == turn["y_halves"]:
                            e1_y_lo(row)
                    else:
                        e = o + NB * (sweep - 2)
                        if at == turn["take"]:
                            acc = acc_b[:, (row + 1) % 2, :] if sweep == 2 else ACC3[o % 4]
                            g_take(e, row, end, acc, sums_of.get((row, sweep), 0))
                        if at == turn["sigmoid"]:
                            g_argument(e)
                        if at == turn["tanh"]:
                            g_state(e, row, sweep == 3)
                        if sweep == 2 and at == turn["y_halves"]:
                            g_y_lo(e, row)
                if t - 1 in closed:
                    take_aside(*closed[t - 1], t - 1)
                if t < T_END:
                    split(t)

        @block.gpsimd
        def _(pool):
            for b in range(BATCHES):
                if b + 1 < BATCHES:
                    pool.wait_ge(y1_mean, b + 2)
                    if b == 0:
                        pool.wait_ge(y1_dev, 1)
                    nc.gpsimd.tensor_tensor(scratch(b + 1, 0), rows_of(x1, b + 1), spread(stat(b + 1, 1)),
                                            ALU.add).then_inc(y1_dev, 1)
                pool.wait_ge(y1_hi, b + 1)
                for k in range(NB - 1 - BATCH * b, NB - 1 - BATCH * (b + 1), -1):
                    nc.gpsimd.tensor_tensor(ya[:, k, :, C:], hall[:, k, :, :],
                                            ya[:, k, :, :C].bitcast(f32), ALU.subtract).then_inc(y1_ready, 1)
            pool.wait_ge(y1_ready, NB)
            with pool.Fori(0, NB) as e:
                pool.wait_ge(h_ready, BATCHES + e + 1)
                pool.sem_inc(past_pool, 1)
                nc.gpsimd.tensor_copy(hall[:, e, :, :], hs[:, :, :]).then_inc(e1_kept, 1)

            def fetch(e, row):
                nc.gpsimd.tensor_copy(hs[:, :, :], hall[:, row, :, :]).then_inc(g_old, 1)
            pool.wait_ge(e1_kept, NB)
            pool.wait_ge(e1_t, NB)
            fetch(0, NB - 1)
            with pool.Fori(0, NB - 1) as e:
                pool.wait_ge(g_h, e + 1)
                pool.sem_inc(past_pool, 1)
                nc.gpsimd.tensor_copy(hall[:, NB - 1 - e, :, :], hs[:, :, :]).then_inc(g_kept, 1)
                pool.wait_ge(g_kept, e + 1)
                pool.sem_inc(past_pool, 1)
                pool.wait_ge(g_t, e + 1)
                pool.sem_inc(past_pool, 1)
                fetch(e + 1, NB - 2 - e)
            pool.wait_ge(g_h, NB)
            nc.gpsimd.tensor_copy(hall[:, 0, :, :], hs[:, :, :]).then_inc(g_kept, 1)
            pool.wait_ge(g_kept, NB)
            pool.wait_ge(g_t, NB)
            order = [row for row, *_ in rows(3)]
            fetch(NB, order[0])

            def store(row):
                pool.dma_start(out[row, :, :], x1[:, row, :, :]).then_inc(stored, 16)

            for o in range(1, NB):
                pool.wait_ge(g_h, NB + o)
                fetch(NB + o, order[o])
                store(order[o - 1])

        @block.tensor
        def _(pe):
            pe.sem_inc(used, SPL)

            def product(t, parts):
                for u in range(UNITS):
                    slot = (UNITS * t + u) % SPL
                    pe.wait_ge(lo_ready, UNITS * (t + RAW) + u + 1)
                    for i in range(KT // UNITS):
                        kt = KT // UNITS * u + i
                        for y, k, acc, opens, closes in parts:
                            for half in (hi, lo):
                                last = nc.tensor.matmul(acc, y[:, k, kt, :], half[:, slot, i * B:(i + 1) * B],
                                                        start=opens and kt == 0 and half is hi,
                                                        stop=closes and kt == KT - 1 and half is lo)
                    last.then_inc(used, 1)

            def transpose_state(sem_done):
                for i in range(KT):
                    last = nc.tensor.transpose(ps_t[:C, i * P:(i + 1) * P], hs[:, i, :], ident[:, :])
                last.then_inc(sem_done, 1)

            def times(dst, lhs, rows, w, sem_done):
                for i in range(KT):
                    last = nc.tensor.matmul(dst[:, i, :C], lhs[:rows, i * P:(i + 1) * P], w[:rows, :],
                                            start=True, stop=True)
                last.then_inc(sem_done, 1)

            def e1_project(e):
                pe.wait_ge(e1_mt, e + 1)
                times(ps_y, mt, P, w0s, e1_agg)

            def e1_transpose(e):
                pe.wait_ge(h_ready, BATCHES + e + 1)
                transpose_state(e1_t)

            def e1_next(e):
                pe.wait_ge(e1_ht, e + 1)
                times(ps_y, ht, C, w1s, e1_y)

            def g_old_transpose(e):
                pe.wait_ge(g_old, e + 1)
                transpose_state(g_oldt)

            def g_sums(e, layer):
                pe.wait_ge(g_mt, e + 1)
                pe.wait_ge(g_oldht, e + 1)
                for i in range(KT):
                    nc.tensor.matmul(ps_g[:, i, :], ht[:, i * P:(i + 1) * P], wh[layer][:, :], start=True, stop=False)
                    last = nc.tensor.matmul(ps_g[:, i, :3 * C], mt[:, i * P:(i + 1) * P], wi[layer][:, :],
                                            start=False, stop=True)
                last.then_inc(g_gates, 1)

            def g_transpose(e):
                pe.wait_ge(g_h, e + 1)
                transpose_state(g_t)

            def g_next(e):
                pe.wait_ge(g_ht, e + 1)
                times(ps_y, ht, C, w2s, g_y)

            def accumulator(sweep, row, o, product):
                if product == 1:
                    return acc_a[:, row % 2, :]
                if sweep == 3:
                    return ACC3[o % 4]
                if product == 2:
                    return acc_b[:, (row + sweep - 1) % 2, :]
                return acc_a[:, row % 2, :]

            def row_may_begin(sweep, row, o):
                if sweep == 1 and row >= 2:
                    pe.wait_ge(e1_part, row - 1)
                if sweep == 2 and o < 2:
                    pe.wait_ge(e1_part, NB - 1 + o)
                if sweep == 2 and o >= 2:
                    pe.wait_ge(g_part, o - 1)
                if sweep == 3:
                    if o == 0:
                        pe.wait_ge(g_mt, NB - 1)
                    elif o == 1:
                        pe.wait_ge(g_part, NB - 1)
                    elif o == 2:
                        pe.wait_ge(g_mt, NB)
                    elif o == 3:
                        pe.wait_ge(g_part, NB)
                    else:
                        pe.wait_ge(g_mt, NB + o - 3)

            def own_steps(t):
                for sweep, row, o, end, turn, at in ending(t):
                    if sweep == 1:
                        if at == turn["project"]:
                            e1_project(row)
                        if at == turn["turn"]:
                            e1_transpose(row)
                        if at == turn["y"]:
                            e1_next(row)
                    else:
                        e = o + NB * (sweep - 2)
                        if at == turn["old"]:
                            g_old_transpose(e)
                        if at == turn["sums"]:
                            g_sums(e, sweep - 2)
                        if sweep == 2 and at == turn["turn"]:
                            g_transpose(e)
                        if sweep == 2 and at == turn["y"]:
                            g_next(e)

            y2_seen = 0
            y3_seen = 0
            sums_aside = 0
            for v, (sweep, row, t0, blocks_, _) in enumerate(VISITS):
                row_may_begin(sweep, row, v % NB)
                for t, (row_, k, todo) in enumerate(blocks_, t0):
                    parts = []
                    for product_, own, opens, closes in todo:
                        if product_ == 1 and row == 0:
                            pe.wait_ge(y1_ready, NB - k)
                        if product_ == 2 and k + 1 > y2_seen:
                            y2_seen = k + 1
                            pe.wait_ge(y2_ready, y2_seen)
                        if product_ == 3 and NB - k > y3_seen:
                            y3_seen = NB - k
                            pe.wait_ge(y3_ready, y3_seen)
                        if own:
                            acc = accumulator(sweep, row, v % NB, product_)
                        else:
                            acc = acc_c[:, :]
                            if opens and sums_aside:
                                pe.wait_ge(aside_part, sums_aside)
                            sums_aside += opens
                        parts.append((yb if product_ == 2 else ya, k, acc, opens, closes))
                    product(t, parts)
                    if t == NB - 1:
                        pe.wait_ge(consts_in, 16 * 11)
                    own_steps(t)
            for t in range(T_END, T_DONE):
                own_steps(t)


def kernel(x, adj, L0_gnn_weight, L1_gnn_W1, L1_gnn_wih1, L1_gnn_whh1, L1_gnn_bih1, L1_gnn_bhh1,
           L1_gnn_W2, L1_gnn_wih2, L1_gnn_whh2, L1_gnn_bih2, L1_gnn_bhh2):
    import concourse.bacc as bacc
    from concourse.bass_utils import run_bass_kernel_spmd

    def lay(a):
        return np.ascontiguousarray(np.asarray(a))

    def hidden(whh, bih, bhh):
        a = np.zeros((C + 2, G), np.float32)
        whh_t = np.asarray(whh).T
        a[:C, :2 * C] = whh_t[:, :2 * C]
        a[:C, 3 * C:] = whh_t[:, 2 * C:]
        a[C, :3 * C] = np.asarray(bih)
        a[C + 1, :2 * C] = np.asarray(bhh)[:2 * C]
        a[C + 1, 3 * C:] = np.asarray(bhh)[2 * C:]
        return a

    blocks = lay(np.asarray(adj).reshape(NB, B, NB, KT, P).transpose(0, 2, 4, 3, 1)).reshape(NB, NB, P, KT * B)
    arrays = {
        "blocks": blocks,
        "x": lay(np.asarray(x).reshape(NB, KT, P, C).transpose(2, 0, 1, 3)),
        "w0": lay(L0_gnn_weight), "w1": lay(L1_gnn_W1), "w2": lay(L1_gnn_W2),
        "wi1": lay(np.asarray(L1_gnn_wih1).T), "wi2": lay(np.asarray(L1_gnn_wih2).T),
        "wh1": hidden(L1_gnn_whh1, L1_gnn_bih1, L1_gnn_bhh1),
        "wh2": hidden(L1_gnn_whh2, L1_gnn_bih2, L1_gnn_bhh2),
        "ident": np.eye(P, dtype=np.float32),
    }
    nc = bacc.Bacc("TRN2", target_bir_lowering=False, num_devices=1)
    args = [nc.dram_tensor(f"in_{n}", a.shape, mybir.dt.from_np(a.dtype), kind="ExternalInput").ap()
            for n, a in arrays.items()]
    out = nc.dram_tensor("out_x", (NB, P, KT * C), mybir.dt.float32, kind="ExternalOutput").ap()
    build(nc, *args, out)
    r = run_bass_kernel_spmd(nc, [{f"in_{n}": a for n, a in arrays.items()}], core_ids=[0])
    got = r.results[0]["out_x"]
    return got.reshape(NB, P, KT, C).transpose(0, 2, 1, 3).reshape(N, C)
```
